# Optimizing a Trainium2 kernel written in Bass

```python
import numpy as np
import jax
import jax.numpy as jnp

def _softmax(x, axis=-1):
    return jax.nn.softmax(x, axis=axis)

def _gelu(x):
    return jax.nn.gelu(x, approximate=True)

def _silu(x):
    return jax.nn.silu(x)

def _sigmoid(x):
    return jax.nn.sigmoid(x)

def _layernorm(x, axis=-1, eps=1e-05):
    m = jnp.mean(x, axis=axis, keepdims=True)
    v = jnp.var(x, axis=axis, keepdims=True)
    return (x - m) / jnp.sqrt(v + eps)

def _scatter_add(tgt, idx, src, axis=0):
    return tgt.at[idx].add(src)

def _segment_sum(src, seg, n):
    return jax.ops.segment_sum(src, seg, n)
kernel_name = 'mk_rec_standalone_d1_rec_r8_8d88cc'

def setup_inputs(seed: int=0):
    np.random.seed(seed)
    _w = jnp.asarray

    def _rec_inputs():
        import jax
        import jax.numpy as jnp
        _rk = jax.random.key(seed)
        r_x = -0.000125008 + 0.999885 * jax.random.normal(jax.random.fold_in(_rk, 1), (2048, 32, 64), jnp.float32)
        return r_x
    r_x = _rec_inputs()

    def _L0_rec_setup():
        import jax, jax.numpy as jnp
        import numpy as np
        B, N_FEAT, D = (2048, 32, 64)
        HID1, HID2, HOF = (1024, 512, 64)
        OUT = 1
        N_PAIRS = N_FEAT * (N_FEAT - 1) // 2
        EPS = 1e-05

        def _batchnorm(h, g, beta):
            m = jnp.mean(h, axis=0)
            v = jnp.var(h, axis=0)
            return g * (h - m) * jax.lax.rsqrt(v + EPS) + beta
        _IU, _JU = np.triu_indices(N_FEAT, k=1)
        key = jax.random.key(seed)
        ks = jax.random.split(key, 16)
        s = 0.02
        return {'x': jax.random.normal(ks[0], (B, N_FEAT, D), dtype=jnp.float32), 'W1': jax.random.normal(ks[1], (N_FEAT * D, HID1), dtype=jnp.float32) * s, 'b1': jnp.zeros((HID1,), jnp.float32), 'g1': jnp.ones((HID1,), jnp.float32), 'beta1': jnp.zeros((HID1,), jnp.float32), 'W2': jax.random.normal(ks[2], (HID1, HID2), dtype=jnp.float32) * s, 'b2': jnp.zeros((HID2,), jnp.float32), 'g2': jnp.ones((HID2,), jnp.float32), 'beta2': jnp.zeros((HID2,), jnp.float32), 'W3': jax.random.normal(ks[3], (HID2, HOF), dtype=jnp.float32) * s, 'b3': jnp.zeros((HOF,), jnp.float32), 'Wc': jax.random.normal(ks[4], (HOF + N_PAIRS, OUT), dtype=jnp.float32) * s, 'bc': jnp.zeros((OUT,), jnp.float32)}
    _L0_rec_all = _L0_rec_setup()
    _L0_rec_in = {k: v for k, v in _L0_rec_all.items() if k in ('W1', 'b1', 'g1', 'beta1', 'W2', 'b2', 'g2', 'beta2', 'W3', 'b3', 'Wc', 'bc')}
    del _L0_rec_all
    return {'r_x': r_x, 'L0_rec_W1': _L0_rec_in['W1'], 'L0_rec_b1': _L0_rec_in['b1'], 'L0_rec_g1': _L0_rec_in['g1'], 'L0_rec_beta1': _L0_rec_in['beta1'], 'L0_rec_W2': _L0_rec_in['W2'], 'L0_rec_b2': _L0_rec_in['b2'], 'L0_rec_g2': _L0_rec_in['g2'], 'L0_rec_beta2': _L0_rec_in['beta2'], 'L0_rec_W3': _L0_rec_in['W3'], 'L0_rec_b3': _L0_rec_in['b3'], 'L0_rec_Wc': _L0_rec_in['Wc'], 'L0_rec_bc': _L0_rec_in['bc']}

def reference(r_x, L0_rec_W1, L0_rec_b1, L0_rec_g1, L0_rec_beta1, L0_rec_W2, L0_rec_b2, L0_rec_g2, L0_rec_beta2, L0_rec_W3, L0_rec_b3, L0_rec_Wc, L0_rec_bc):
    import jax
    import jax.numpy as jnp

    def _L0_rec_ref(x, W1, b1, g1, beta1, W2, b2, g2, beta2, W3, b3, Wc, bc):
        import jax, jax.numpy as jnp
        import numpy as np
        B, N_FEAT, D = (2048, 32, 64)
        HID1, HID2, HOF = (1024, 512, 64)
        OUT = 1
        N_PAIRS = N_FEAT * (N_FEAT - 1) // 2
        EPS = 1e-05

        def _batchnorm(h, g, beta):
            m = jnp.mean(h, axis=0)
            v = jnp.var(h, axis=0)
            return g * (h - m) * jax.lax.rsqrt(v + EPS) + beta
        _IU, _JU = np.triu_indices(N_FEAT, k=1)
        gram = jnp.einsum('bnd,bmd->bnm', x, x)
        pairs = gram[:, _IU, _JU]
        flat = x.reshape(x.shape[0], -1)
        h = _batchnorm(jax.nn.relu(flat @ W1 + b1), g1, beta1)
        h = _batchnorm(jax.nn.relu(h @ W2 + b2), g2, beta2)
        hof = h @ W3 + b3
        inter = jnp.concatenate([hof, pairs], axis=1)
        return inter @ Wc + bc
    y = _L0_rec_ref(r_x, L0_rec_W1, L0_rec_b1, L0_rec_g1, L0_rec_beta1, L0_rec_W2, L0_rec_b2, L0_rec_g2, L0_rec_beta2, L0_rec_W3, L0_rec_b3, L0_rec_Wc, L0_rec_bc)
    return y

_drawn_inputs = setup_inputs


def setup_inputs(seed=0):
    import zlib

    import numpy as np

    out = dict(_drawn_inputs(seed))
    spreads = {'L0_rec_b1': (0.0, 2.0),
     'L0_rec_g1': (1.0, 0.6),
     'L0_rec_beta1': (0.0, 2.0),
     'L0_rec_b2': (0.0, 2.0),
     'L0_rec_g2': (1.0, 0.6),
     'L0_rec_beta2': (0.0, 0.8),
     'L0_rec_b3': (0.0, 2.0)}
    factors = {'L0_rec_W1': 2.777, 'L0_rec_W2': 2.77, 'L0_rec_W3': 2.716}
    for name, (base, spread) in spreads.items():
        noise = np.random.default_rng([zlib.crc32(name.encode()), seed]).standard_normal(out[name].shape)
        drawn = base * np.exp(spread * noise) if base else spread * noise
        out[name] = jnp.asarray(drawn.astype(out[name].dtype))
    for name, factor in factors.items():
        out[name] = (out[name] * factor).astype(out[name].dtype)
    return out
```

```python
import concourse.bass as bass
from concourse import mybir
from contextlib import ExitStack

FP32 = mybir.dt.float32
FP32R = mybir.dt.float32r
ALU = mybir.AluOpType
ACT = mybir.ActivationFunctionType
AX = mybir.AxisListType

P = 128
B, NF, D = 2048, 32, 64
F = NF * D
H1, H2, HO = 1024, 512, 64
EPS = 1e-5
NT = 512
TILES = B // NT
KT = F // P
DK = P // NF
HALF = H1 // 2
MT = HALF // P
K2 = H1 // P
M2 = H2 // P
XT_SLOTS = 8
HL_SLOTS = 4
W_STAGE = 4
BLKS = NT // 32
COLS = B // P
LAG = 5


def build(nc, x, W1, b1, g1, beta1, W2, b2, g2, beta2, W3, b3, Wc, bc, out):
    ctx = ExitStack()
    with ctx:
        def sb(name, shape, dt=FP32):
            return ctx.enter_context(nc.sbuf_tensor(name, shape, dt))

        def sem(name):
            return ctx.enter_context(nc.semaphore(name))

        w_hl = sb("w_hl", [P, KT, 2, HALF], FP32R)
        x_hl = sb("x_hl", [P, HL_SLOTS, 2, NT], FP32R)
        xT = sb("xT", [P, XT_SLOTS, NT])
        x_raw = sb("x_raw", [P, BLKS, NT])
        h1 = sb("h1", [P, K2, TILES, NT])
        w_raw = sb("w_raw", [P, W_STAGE, HALF])
        h2 = x_raw[:, :, :].rearrange("p (m n) c -> p m n c", m=M2)
        pair_sum = h1[:, K2 - 1, :, :]
        pair_prod = h1[:, K2 - 2, :, :]
        ident = sb("ident", [P, P])
        ones = sb("ones", [P, P])
        c_raw = sb("c_raw", [P, NF])
        c_mask = sb("c_mask", [P, DK])
        c_full = sb("c_full", [P, NF, DK])
        c_hl = sb("c_hl", [P, 2, P], FP32R)
        NPAR = 3 * K2 + 3 * M2
        par_rows = sb("par_rows", [NPAR, P])
        par = sb("par", [P, NPAR])
        b1_c, g1_c, be1_c = (par[:, i * K2:(i + 1) * K2] for i in range(3))
        b2_c, g2_c, be2_c = (par[:, 3 * K2 + i * M2:3 * K2 + (i + 1) * M2] for i in range(3))
        w3 = sb("w3", [P, M2, HO])
        w3p = sb("w3p", [P, HO])
        wc_b = sb("wc_b", [P, HO])
        b3_b = sb("b3_b", [P, HO])
        bc_b = sb("bc_b", [P, 1])
        w3c = sb("w3c", [P, M2])
        k3 = sb("k3", [P, 1])
        kc = sb("kc", [P, 1])
        st1 = sb("st1", [P, K2, TILES, 6])
        st2 = sb("st2", [P, M2, TILES, 6])
        mv1 = sb("mv1", [P, K2, 2])
        mv2 = sb("mv2", [P, M2, 2])
        ve = sb("ve", [P, K2])
        sd = sb("sd", [P, K2])
        r0 = sb("r0", [P, K2])
        nt = sb("nt", [P, K2])
        a1 = sb("a1", [P, K2])
        c1 = sb("c1", [P, K2])
        b2f = sb("b2f", [P, M2])
        a2 = sb("a2", [P, M2])
        v2 = sb("v2", [P, M2])
        s2 = sb("s2", [P, M2])
        s2s = sb("s2s", [P, 1])
        y_pair = sb("y_pair", [P, COLS])
        y_sb = sb("y_sb", [P, COLS])

        ps = [ctx.enter_context(nc.psum_tensor(f"ps{i}", [P, NT], FP32)) for i in range(8)]
        ps_y, ps_m = ps[6], ps[7]
        ps_par = ps_m[:, 0:NPAR]
        ps_b2 = ps_m[:, 64:64 + M2]
        ps_k = ps_m[:, 96:97]

        x_loaded = sem("x_loaded")
        w_loaded = [sem(f"w_loaded{i}") for i in range(W_STAGE)]
        w2b_loaded = sem("w2b_loaded")
        c_loaded = sem("c_loaded")
        par_loaded = sem("par_loaded")
        l3_loaded = sem("l3_loaded")
        y_stored = sem("y_stored")
        pool_set = sem("pool_set")
        par_turned = sem("par_turned")
        par_ready = sem("par_ready")
        c_split = sem("c_split")
        c_built = sem("c_built")
        turned = sem("turned")
        x_hi = sem("x_hi")
        x_lo = sem("x_lo")
        w_hi = sem("w_hi")
        w_lo = sem("w_lo")
        pe_steps = sem("pe_steps")
        m_done = sem("m_done")
        prod_done = sem("prod_done")
        sum_done = sem("sum_done")
        h1_ready = sem("h1_ready")
        st1_done = sem("st1_done")
        yp_done = sem("yp_done")
        yp_saved = sem("yp_saved")
        ve_ready = sem("ve_ready")
        sd_ready = sem("sd_ready")
        a1_ready = sem("a1_ready")
        w2_hi = sem("w2_hi")
        w2_lo = sem("w2_lo")
        h_hi = sem("h_hi")
        h_lo = sem("h_lo")
        pe_steps2 = sem("pe_steps2")
        b2_done = sem("b2_done")
        b2_ready = sem("b2_ready")
        m2_done = sem("m2_done")
        h2_ready = sem("h2_ready")
        v2_ready = sem("v2_ready")
        s2_ready = sem("s2_ready")
        y_done = sem("y_done")
        y_ready = sem("y_ready")
        dve_chain = sem("dve_chain")

        x_v = x.rearrange("(g j c) i d -> c g j (i d)", g=4, j=32)
        w1_v = W1.rearrange("(i t e) n -> t i e n", t=KT, e=DK)
        steps = TILES * KT
        VE = [K2 // 2, K2 // 2, M2 - 1, 1]

        block = ctx.enter_context(nc.Block())

        @block.sync
        def _(sp):
            def load_x(n):
                for q in range(4):
                    for cc in range(4):
                        src = x_v[n * 4 + cc, :, :, q * NT:(q + 1) * NT].rearrange("g j f -> j g f")
                        sp.dma_start(x_raw[32 * q:32 * q + 32, 4 * cc:4 * cc + 4, :], src).then_inc(x_loaded, 16)

            def load_w1(s, k):
                if s or k >= W_STAGE:
                    sp.wait_ge(w_hi, s * KT + k - W_STAGE + 1)
                    sp.wait_ge(w_lo, s * KT + k - W_STAGE + 1)
                sp.dma_start(w_raw[:, k % W_STAGE, :],
                             w1_v[k, :, :, s * HALF:(s + 1) * HALF]).then_inc(w_loaded[k % W_STAGE], 16)

            for s in range(2):
                if s:
                    sp.wait_ge(turned, steps)
                load_x(0)
                for k in range(KT):
                    load_w1(s, k)
                with sp.Fori(1, TILES) as n:
                    sp.wait_ge(turned, n * KT + s * steps)
                    load_x(n)
            for k in range(K2 // 2):
                sp.wait_ge(w_hi, KT + KT - W_STAGE + k + 1)
                sp.wait_ge(w_lo, KT + KT - W_STAGE + k + 1)
                sp.dma_start(w_raw[:, k, :], W2[k * P:(k + 1) * P, :]).then_inc(w_loaded[k], 16)
            sp.wait_ge(x_hi, 2 * steps)
            sp.wait_ge(x_lo, 2 * steps)
            sp.dma_start(xT[:, 0:K2 // 2, :],
                         W2[H1 // 2:H1, :].rearrange("(k p) n -> p k n", p=P)).then_inc(w2b_loaded, 16)
            sp.wait_ge(y_ready, 1)
            sp.dma_start(out.rearrange("(p c) o -> p (c o)", c=COLS), y_sb[:, :]).then_inc(y_stored, 16)
            sp.wait_ge(y_stored, 16)

        @block.gpsimd
        def _(pool):
            pool.memset(c_raw[:, :], 0.0).then_inc(pool_set, 1)
            pool.memset(ident[:, :], 0.0).then_inc(pool_set, 1)
            pool.memset(ones[:, :], 1.0).then_inc(pool_set, 1)
            pool.wait_ge(pool_set, 3)
            pool.affine_select(out=ident[:, :], in_=ident[:, :], compare_op=ALU.not_equal, fill=1.0, base=0,
                               pattern=[[-1, P]], channel_multiplier=1).then_inc(pool_set, 1)
            for s in range(2):
                for k in range(KT):
                    pool.wait_ge(w_loaded[k % W_STAGE], 16 * (s * KT // W_STAGE + k // W_STAGE + 1))
                    pool.wait_ge(w_hi, s * KT + k + 1)
                    if s:
                        pool.wait_ge(pe_steps, steps - KT + k + 1)
                    pool.tensor_tensor(w_hl[:, k, 1, :], w_raw[:, k % W_STAGE, :],
                                       w_hl[:, k, 0, :].bitcast(FP32), ALU.subtract).then_inc(w_lo, 1)

        @block.scalar
        def _(act):
            act.wait_ge(pool_set, 3)
            for i in range(NF - 1):
                at = HO + i * (2 * NF - i - 1) // 2
                src = Wc[at:at + NF - 1 - i, :].rearrange("a o -> o a").to_broadcast([DK, NF - 1 - i])
                act.dma_start(c_raw[DK * i:DK * i + DK, i + 1:NF], src).then_inc(c_loaded, 16)
            for i, v in enumerate((b1, g1, beta1)):
                act.dma_start(par_rows[i * K2:(i + 1) * K2, :],
                              v.rearrange("(m p) -> m p", p=P)).then_inc(par_loaded, 16)
            for i, v in enumerate((b2, g2, beta2)):
                act.dma_start(par_rows[3 * K2 + i * M2:3 * K2 + (i + 1) * M2, :],
                              v.rearrange("(m p) -> m p", p=P)).then_inc(par_loaded, 16)
            act.dma_start(w3[:, :, :], W3.rearrange("(m p) h -> p m h", p=P)).then_inc(l3_loaded, 16)
            act.dma_start(wc_b[:, :], Wc[0:HO, :].rearrange("a o -> o a").to_broadcast([P, HO])).then_inc(l3_loaded, 16)
            act.dma_start(b3_b[:, :], b3.rearrange("(o a) -> o a", o=1).to_broadcast([P, HO])).then_inc(l3_loaded, 16)
            act.dma_start(bc_b[:, :], bc.rearrange("(o a) -> o a", o=1).to_broadcast([P, 1])).then_inc(l3_loaded, 16)
            act.wait_ge(c_built, 1)
            act.copy(c_hl[:, 0, :], c_full[:, :, :].rearrange("p j e -> p (j e)")).then_inc(c_split, 1)

            def hi_of_w1(s, k):
                act.wait_ge(w_loaded[k % W_STAGE], 16 * (s * KT // W_STAGE + k // W_STAGE + 1))
                if s:
                    act.wait_ge(pe_steps, steps - KT + k + 1)
                act.copy(w_hl[:, k, 0, :], w_raw[:, k % W_STAGE, :]).then_inc(w_hi, 1)

            def hi_of_x(u, k, first):
                act.wait_ge(turned, u * KT + k + 1)
                if not (first and k < HL_SLOTS):
                    act.wait_ge(pe_steps, u * KT + k - HL_SLOTS + 1)
                act.copy(x_hl[:, k % HL_SLOTS, 0, :], xT[:, k % XT_SLOTS, :]).then_inc(x_hi, 1)

            def relu1(s, u, n):
                for m in range(MT):
                    if m < MT - 1:
                        act.wait_ge(m_done, (u - 1) * (MT - 1) + m + 1)
                    else:
                        act.wait_ge(pe_steps, u * KT)
                    act.activation(h1[:, s * MT + m, n, :], ps[m][:, :], ACT.Relu,
                                   bias=b1_c[:, s * MT + m:s * MT + m + 1]).then_inc(h1_ready, 1)

            for s in range(2):
                for k in range(KT):
                    if s and k == HL_SLOTS - 1:
                        relu1(0, TILES, TILES - 1)
                    hi_of_w1(s, k)
                    hi_of_x(s * TILES, k, s == 0)
                with act.Fori(1, TILES) as n:
                    u = n + s * TILES
                    for k in range(KT):
                        if k == HL_SLOTS - 1:
                            if s == 0:
                                act.wait_ge(par_ready, 1)
                            else:
                                act.wait_ge(yp_saved, 1)
                            relu1(s, u, n - 1)
                        hi_of_x(u, k, False)

            def root(n):
                act.wait_ge(ve_ready, n + 1)
                act.activation(sd[:, 0:VE[n]], ve[:, 0:VE[n]], ACT.Sqrt).then_inc(sd_ready, 1)

            def hi_of_w2(k):
                act.wait_ge(a1_ready, 1 + k // (K2 // 2))
                if k < K2 // 2:
                    act.wait_ge(w_loaded[k], 16 * (2 * KT // W_STAGE + 1))
                    act.wait_ge(pe_steps, 2 * steps - KT + K2)
                    src = w_raw[:, k, :]
                else:
                    act.wait_ge(w2b_loaded, 16)
                    src = xT[:, k - K2 // 2, :]
                act.activation(w_hl[:, k, 0, :], src, ACT.Copy, scale=a1[:, k:k + 1]).then_inc(w2_hi, 1)

            def hi_of_h1(n, k, first):
                if first:
                    act.wait_ge(pe_steps, 2 * steps - KT + K2 + k + 1)
                    if k >= K2 // 2:
                        act.wait_ge(h1_ready, 2 * TILES * MT)
                else:
                    act.wait_ge(pe_steps2, (n - 1) * K2 + k + 1)
                act.copy(w_hl[:, K2 + k, 0, :], h1[:, k, n, :]).then_inc(h_hi, 1)

            def relu2(n):
                for m in range(M2):
                    if m < M2 - 1:
                        act.wait_ge(m2_done, n * (M2 - 1) + m + 1)
                    else:
                        act.wait_ge(pe_steps2, (n + 1) * K2)
                    act.activation(h2[:, m, n, :], ps[m][:, :], ACT.Relu, bias=b2f[:, m:m + 1]).then_inc(h2_ready, 1)

            root(0)
            for k in range(K2 // 2):
                hi_of_w2(k)
            for k in range(K2 // 2):
                hi_of_h1(0, k, True)
            relu1(1, 2 * TILES, TILES - 1)
            for k in range(K2 // 2, K2):
                hi_of_h1(0, k, True)
            root(1)
            for k in range(K2 // 2, K2):
                hi_of_w2(k)
            act.wait_ge(b2_ready, 1)
            with act.Fori(1, TILES) as n:
                for k in range(K2):
                    if k == K2 - 1:
                        relu2(n - 1)
                    hi_of_h1(n, k, False)
            for m in range(M2):
                act.wait_ge(m2_done, (TILES - 1) * (M2 - 1) + m + 1)
                act.activation(h2[:, m, TILES - 1, :], ps[m][:, :], ACT.Relu, bias=b2f[:, m:m + 1]).then_inc(h2_ready, 1)
                if m >= M2 - 2:
                    root(m - M2 + 4)

        @block.tensor
        def _(pe):
            pe.wait_ge(pool_set, 4)
            pe.wait_ge(par_loaded, 96)
            pe.transpose(ps_par, par_rows[:, :], ident[0:NPAR, 0:NPAR]).then_inc(par_turned, 1)

            def three(acc, w_hi_ap, w_lo_ap, x_hi_ap, x_lo_ap, start, stop):
                pe.matmul(acc, w_hi_ap, x_hi_ap, start=start, stop=False)
                pe.matmul(acc, w_hi_ap, x_lo_ap, start=False, stop=False)
                return pe.matmul(acc, w_lo_ap, x_hi_ap, start=False, stop=stop)

            def step1(s, u, k, first_in_sweep):
                hi, lo = x_hl[:, k % HL_SLOTS, 0, :], x_hl[:, k % HL_SLOTS, 1, :]
                pe.wait_ge(x_hi, u * KT + k + 1)
                pe.wait_ge(x_lo, u * KT + k + 1)
                if first_in_sweep:
                    pe.wait_ge(w_hi, s * KT + k + 1)
                    pe.wait_ge(w_lo, s * KT + k + 1)
                for m in range(MT):
                    if k == 0 and not (s == 0 and first_in_sweep):
                        pe.wait_ge(h1_ready, (u - 1) * MT + m + 1)
                    cols = slice(m * P, (m + 1) * P)
                    mm = three(ps[m][:, :], w_hl[:, k, 0, cols], w_hl[:, k, 1, cols], hi, lo, k == 0, k == KT - 1)
                    if k == KT - 1 and m < MT - 1:
                        mm.then_inc(m_done, 1)
                if s == 0:
                    if first_in_sweep and k == 0:
                        pe.wait_ge(c_split, 2)
                    if not (first_in_sweep and k < 2):
                        pe.wait_ge(prod_done, u * KT + k - 1)
                    mm = three(ps[4 + k % 2][:, :], c_hl[:, 0, :], c_hl[:, 1, :], hi, lo, True, True)
                mm.then_inc(pe_steps, 1)

            for s in range(2):
                for k in range(KT):
                    step1(s, s * TILES, k, True)
                    if s and k == 7:
                        pe.wait_ge(sum_done, TILES * (KT - 1))
                        for c in range(COLS):
                            mm = pe.matmul(ps_y[:, c:c + 1], pair_sum[:, c // 4, (c % 4) * P:(c % 4 + 1) * P],
                                           ones[:, 0:1], start=True, stop=True)
                        mm.then_inc(yp_done, 1)
                with pe.Fori(1, TILES) as n:
                    for k in range(KT):
                        step1(s, n + s * TILES, k, False)

            def step2(n, k, first, m_from=0, m_to=M2):
                pe.wait_ge(h_hi, n * K2 + k + 1)
                pe.wait_ge(h_lo, n * K2 + k + 1)
                if first:
                    pe.wait_ge(w2_hi, k + 1)
                    pe.wait_ge(w2_lo, k + 1)
                for m in range(m_from, m_to):
                    if k == 0:
                        if first:
                            pe.wait_ge(h1_ready, (2 * TILES - 1) * MT + m + 1)
                        else:
                            pe.wait_ge(h2_ready, (n - 1) * M2 + m + 1)
                    cols = slice(m * P, (m + 1) * P)
                    mm = three(ps[m][:, :], w_hl[:, k, 0, cols], w_hl[:, k, 1, cols],
                               w_hl[:, K2 + k, 0, :], w_hl[:, K2 + k, 1, :], k == 0, k == K2 - 1)
                    if k == K2 - 1 and (m < M2 - 1 or m_from):
                        mm.then_inc(m2_done, 1)
                    elif m == M2 - 1 and not m_from:
                        mm.then_inc(pe_steps2, 1)

            for k in range(K2):
                step2(0, k, True)
                if k == K2 // 2:
                    pe.wait_ge(a1_ready, 2)
                    for m in range(M2):
                        for kk in range(K2):
                            w = w_raw[:, kk, m * P:(m + 1) * P] if kk < K2 // 2 else \
                                xT[:, kk - K2 // 2, m * P:(m + 1) * P]
                            mm = pe.matmul(ps_b2[:, m:m + 1], w, c1[:, kk:kk + 1], start=(kk == 0), stop=(kk == K2 - 1))
                    mm.then_inc(b2_done, 1)
            with pe.Fori(1, TILES - 1) as n:
                for k in range(K2):
                    step2(n, k, False)
            for m in range(M2):
                for k in range(K2):
                    step2(TILES - 1, k, False, m, m + 1)
            pe.wait_ge(yp_saved, 1)
            for m in range(M2):
                pe.wait_ge(v2_ready, 1 if m < M2 - 1 else 2)
                for c in range(COLS):
                    mm = pe.matmul(ps_y[:, c:c + 1], h2[:, m, c // 4, (c % 4) * P:(c % 4 + 1) * P], v2[:, m:m + 1],
                                   start=(m == 0 and c == 0), stop=(m == M2 - 1), skip_group_check=True)
            mm.then_inc(y_done, 1)
            pe.wait_ge(s2_ready, 1)
            pe.matmul(ps_k, ones[:, :], s2s[:, :], start=True, stop=True).then_inc(y_done, 1)

        @block.vector
        def _(dve):
            chain = [0]

            def link(ins):
                chain[0] += 1
                ins.then_inc(dve_chain, 1)
                dve.wait_ge(dve_chain, chain[0])

            dve.wait_ge(pool_set, 4)
            link(dve.tensor_reduce(c_mask[:, :], ident[:, :].rearrange("p (i e) -> p e i", e=DK), AX.X, ALU.max))
            dve.wait_ge(c_loaded, 16 * (NF - 1))
            for e in range(DK):
                last = dve.tensor_scalar(c_full[:, :, e], c_raw[:, :], c_mask[:, e:e + 1], None, ALU.mult)
            last.then_inc(c_built, 1)
            dve.wait_ge(c_split, 1)
            dve.tensor_tensor(c_hl[:, 1, :], c_full[:, :, :].rearrange("p j e -> p (j e)"),
                              c_hl[:, 0, :].bitcast(FP32), ALU.subtract).then_inc(c_split, 1)

            def turn(u, k, first):
                if k == 0:
                    dve.wait_ge(x_loaded, (u + 1) * 256)
                if not (first and k < XT_SLOTS):
                    dve.wait_ge(x_hi, u * KT + k - XT_SLOTS + 1)
                dve.transpose(xT[:, k % XT_SLOTS, :],
                              x_raw[:, :, :].rearrange("p b (i d) -> p b i d", d=D)[:, :, :, DK * k:DK * k + DK]
                              ).then_inc(turned, 1)

            def lo_of_x(u, k, first):
                dve.wait_ge(x_hi, u * KT + k + 1)
                if not (first and k < HL_SLOTS):
                    dve.wait_ge(pe_steps, u * KT + k - HL_SLOTS + 1)
                dve.tensor_tensor(x_hl[:, k % HL_SLOTS, 1, :], xT[:, k % XT_SLOTS, :],
                                  x_hl[:, k % HL_SLOTS, 0, :].bitcast(FP32), ALU.subtract).then_inc(x_lo, 1)

            def product(n, k):
                dve.wait_ge(pe_steps, n * KT + k + 1)
                dst = pair_sum[:, n, :] if k == 0 else pair_prod[:, k % 4, :]
                dve.tensor_tensor(dst, ps[4 + k % 2][:, :], xT[:, k % XT_SLOTS, :], ALU.mult).then_inc(prod_done, 1)

            def add_up(n, k):
                dve.wait_ge(prod_done, n * KT + k + 1)
                if k >= 2:
                    dve.wait_ge(sum_done, n * (KT - 1) + k - 1)
                dve.tensor_tensor(pair_sum[:, n, :], pair_sum[:, n, :], pair_prod[:, k % 4, :],
                                  ALU.add).then_inc(sum_done, 1)

            def stats1(s, u, n, m):
                dve.wait_ge(h1_ready, (u - 1) * MT + m + 1)
                dve.bn_stats(st1[:, s * MT + m, n, :], h1[:, s * MT + m, n, :]).then_inc(st1_done, 1)

            def steps_of(s, u, n, first, pairs_before, pairs_now):
                for k in range(KT):
                    turn(u, k, first and s == 0)
                    if k >= 1:
                        lo_of_x(u, k - 1, first and s == 0)
                    elif not (first and s == 0):
                        lo_of_x(u - 1, KT - 1, False)
                    if k < LAG and pairs_before:
                        product(n - 1, KT + k - LAG)
                    if k <= LAG and pairs_before:
                        add_up(n - 1, KT + k - LAG - 1)
                    if k >= LAG and pairs_now:
                        product(n, k - LAG)
                    if k >= LAG + 2 and pairs_now:
                        add_up(n, k - LAG - 1)
                    if not (first and s == 0) and HL_SLOTS + 1 <= k < HL_SLOTS + 1 + MT:
                        if first:
                            stats1(s - 1, u, TILES - 1, k - HL_SLOTS - 1)
                        else:
                            stats1(s, u, n - 1, k - HL_SLOTS - 1)

            def fold_scale(g, be, mv, a, c, lo, hi, batch):
                w = hi - lo
                dve.tensor_scalar(ve[:, 0:w], mv[:, lo:hi, 1], EPS, None, ALU.add).then_inc(ve_ready, 1)
                dve.wait_ge(sd_ready, batch + 1)
                link(dve.reciprocal(r0[:, 0:w], sd[:, 0:w]))
                link(dve.tensor_tensor(nt[:, 0:w], r0[:, 0:w], r0[:, 0:w], ALU.mult))
                link(dve.tensor_tensor(nt[:, 0:w], nt[:, 0:w], ve[:, 0:w], ALU.mult))
                link(dve.tensor_scalar(nt[:, 0:w], nt[:, 0:w], -0.5, 1.5, ALU.mult, ALU.add))
                link(dve.tensor_tensor(nt[:, 0:w], nt[:, 0:w], r0[:, 0:w], ALU.mult))
                link(dve.tensor_tensor(a[:, lo:hi], nt[:, 0:w], g[:, lo:hi], ALU.mult))
                link(dve.tensor_tensor(nt[:, 0:w], mv[:, lo:hi, 0], a[:, lo:hi], ALU.mult))
                return dve.tensor_tensor(c[:, lo:hi], be[:, lo:hi], nt[:, 0:w], ALU.subtract)

            def lo_of_w2(k):
                dve.wait_ge(w2_hi, k + 1)
                src = w_raw[:, k, :] if k < K2 // 2 else xT[:, k - K2 // 2, :]
                dve.scalar_tensor_tensor(w_hl[:, k, 1, :], src, a1[:, k:k + 1], w_hl[:, k, 0, :].bitcast(FP32),
                                         ALU.mult, ALU.subtract).then_inc(w2_lo, 1)

            def lo_of_h1(n, k):
                dve.wait_ge(h_hi, n * K2 + k + 1)
                dve.tensor_tensor(w_hl[:, K2 + k, 1, :], h1[:, k, n, :], w_hl[:, K2 + k, 0, :].bitcast(FP32),
                                  ALU.subtract).then_inc(h_lo, 1)

            for s in range(2):
                steps_of(s, s * TILES, TILES if s else 0, True, s == 1, s == 0)
                if s == 0:
                    dve.wait_ge(par_turned, 1)
                    dve.tensor_copy(par[:, :], ps_par).then_inc(par_ready, 1)
                    dve.wait_ge(l3_loaded, 64)
                    for m in range(M2):
                        link(dve.tensor_tensor(w3p[:, :], w3[:, m, :], wc_b[:, :], ALU.mult))
                        link(dve.tensor_reduce(w3c[:, m:m + 1], w3p[:, :], AX.X, ALU.add))
                    link(dve.tensor_tensor(w3p[:, :], b3_b[:, :], wc_b[:, :], ALU.mult))
                    link(dve.tensor_reduce(k3[:, :], w3p[:, :], AX.X, ALU.add))
                    link(dve.tensor_tensor(k3[:, :], k3[:, :], bc_b[:, :], ALU.add))
                else:
                    dve.wait_ge(yp_done, 1)
                    dve.tensor_copy(y_pair[:, :], ps_y[:, 0:COLS]).then_inc(yp_saved, 1)
                with dve.Fori(1, TILES) as n:
                    steps_of(s, n + s * TILES, n, False, s == 0, s == 0)
            lo_of_x(2 * TILES - 1, KT - 1, False)

            dve.wait_ge(st1_done, TILES * MT)
            for m in range(MT):
                link(dve.bn_aggr(mv1[:, m, :], st1[:, m, :, :].rearrange("p t s -> p (t s)")))
            fold_scale(g1_c, be1_c, mv1, a1, c1, 0, MT, 0).then_inc(a1_ready, 1)
            for k in range(K2 // 2):
                lo_of_w2(k)
            for k in range(K2 // 2):
                lo_of_h1(0, k)
            for m in range(MT):
                stats1(1, 2 * TILES, TILES - 1, m)
            dve.wait_ge(st1_done, 2 * TILES * MT)
            for m in range(MT, K2):
                link(dve.bn_aggr(mv1[:, m, :], st1[:, m, :, :].rearrange("p t s -> p (t s)")))
            fold_scale(g1_c, be1_c, mv1, a1, c1, MT, K2, 1).then_inc(a1_ready, 1)
            for k in range(K2 // 2, K2):
                lo_of_w2(k)
                lo_of_h1(0, k)
            dve.wait_ge(b2_done, 1)
            dve.tensor_tensor(b2f[:, :], ps_b2, b2_c, ALU.add).then_inc(b2_ready, 1)

            def stats2(n, m):
                dve.wait_ge(h2_ready, n * M2 + m + 1)
                return dve.bn_stats(st2[:, m, n, :], h2[:, m, n, :])

            with dve.Fori(1, TILES) as n:
                for k in range(K2 - 1):
                    lo_of_h1(n, k)
                for m in range(M2):
                    stats2(n - 1, m)
                lo_of_h1(n, K2 - 1)

            def norm2(lo, hi, batch):
                for m in range(lo, hi):
                    link(stats2(TILES - 1, m))
                    link(dve.bn_aggr(mv2[:, m, :], st2[:, m, :, :].rearrange("p t s -> p (t s)")))
                link(fold_scale(g2_c, be2_c, mv2, a2, s2, lo, hi, batch))
                dve.tensor_tensor(v2[:, lo:hi], a2[:, lo:hi], w3c[:, lo:hi], ALU.mult).then_inc(v2_ready, 1)
                link(dve.tensor_tensor(s2[:, lo:hi], s2[:, lo:hi], w3c[:, lo:hi], ALU.mult))

            norm2(0, M2 - 1, 2)
            norm2(M2 - 1, M2, 3)
            dve.tensor_reduce(s2s[:, :], s2[:, :], AX.X, ALU.add).then_inc(s2_ready, 1)
            dve.wait_ge(y_done, 2)
            link(dve.tensor_tensor(kc[:, :], k3[:, :], ps_k, ALU.add))
            dve.scalar_tensor_tensor(y_sb[:, :], ps_y[:, 0:COLS], kc[:, 0:1], y_pair[:, :], ALU.add,
                                     ALU.add).then_inc(y_ready, 1)


_INS = ['r_x', 'L0_rec_W1', 'L0_rec_b1', 'L0_rec_g1', 'L0_rec_beta1', 'L0_rec_W2', 'L0_rec_b2', 'L0_rec_g2',
        'L0_rec_beta2', 'L0_rec_W3', 'L0_rec_b3', 'L0_rec_Wc', 'L0_rec_bc']
_OUTS = [((B, 1), 'float32')]


def kernel(**inputs):
    import numpy as _np
    import concourse.bacc as _bacc
    from concourse import mybir as _mybir
    from concourse.bass_utils import run_bass_kernel_spmd as _run

    nc = _bacc.Bacc("TRN2", target_bir_lowering=False, num_devices=1)
    arrays, args = {}, []
    for name in _INS:
        a = _np.ascontiguousarray(inputs[name])
        arrays[f"in_{name}_dram"] = a
        args.append(nc.dram_tensor(f"in_{name}_dram", a.shape, _mybir.dt.from_np(a.dtype), kind="ExternalInput").ap())
    for i, (shape, dtype) in enumerate(_OUTS):
        dt = _mybir.dt.from_np(_np.dtype(dtype))
        args.append(nc.dram_tensor(f"out_{i}_dram", shape, dt, kind="ExternalOutput").ap())
    build(nc, *args)
    r = _run(nc, [arrays], core_ids=[0])
    got = tuple(r.results[0][f"out_{i}_dram"] for i in range(len(_OUTS)))
    return got[0]
```

```python
import concourse.bass as bass
from concourse import mybir
from contextlib import ExitStack

FP32 = mybir.dt.float32
FP32R = mybir.dt.float32r
ALU = mybir.AluOpType
ACT = mybir.ActivationFunctionType
AX = mybir.AxisListType

P = 128
B, NF, D = 2048, 32, 64
F = NF * D
H1, H2, HO = 1024, 512, 64
EPS = 1e-5
NT = 512
TILES = B // NT
KT = F // P
DK = P // NF
HALF = H1 // 2
MT = HALF // P
K2 = H1 // P
M2 = H2 // P
XT_SLOTS = 8
HL_SLOTS = 4
W_STAGE = 4
BLKS = NT // 32
COLS = B // P
LAG = HL_SLOTS
TURNED_EARLY = KT // 2


def build(nc, x, W1, b1, g1, beta1, W2, b2, g2, beta2, W3, b3, Wc, bc, out):
    ctx = ExitStack()
    with ctx:
        def sb(name, shape, dt=FP32):
            return ctx.enter_context(nc.sbuf_tensor(name, shape, dt))

        def sem(name):
            return ctx.enter_context(nc.semaphore(name))

        w_hl = sb("w_hl", [P, KT, 2, HALF], FP32R)
        x_hl = sb("x_hl", [P, HL_SLOTS, 2, NT], FP32R)
        xT = sb("xT", [P, XT_SLOTS, NT])
        x_raw = sb("x_raw", [P, BLKS, NT])
        h1 = sb("h1", [P, K2, TILES, NT])
        w_raw = sb("w_raw", [P, W_STAGE, HALF])
        h2 = x_raw[:, :, :].rearrange("p (m t) (q n j) -> p m (t q) n j", m=M2, n=TILES, j=32)
        pair_sum = h1[:, K2 - 1, :, :].rearrange("p t (q n j) -> p (t q) n j", n=TILES, j=32)
        pair_prod = h1[:, K2 - 2, :, :]
        ident = sb("ident", [P, P])
        ones = sb("ones", [P, P])
        c_raw = sb("c_raw", [P, NF])
        c_mask = sb("c_mask", [P, DK])
        c_full = sb("c_full", [P, NF, DK])
        c_hl = sb("c_hl", [P, 2, P], FP32R)
        NPAR = 3 * K2 + 3 * M2
        par_rows = sb("par_rows", [NPAR, P])
        par = sb("par", [P, NPAR])
        b1_c, g1_c, be1_c = (par[:, i * K2:(i + 1) * K2] for i in range(3))
        b2_c, g2_c, be2_c = (par[:, 3 * K2 + i * M2:3 * K2 + (i + 1) * M2] for i in range(3))
        w3 = sb("w3", [P, M2, HO])
        w3p = sb("w3p", [P, HO])
        wc_b = sb("wc_b", [P, HO])
        b3_b = sb("b3_b", [P, HO])
        bc_b = sb("bc_b", [P, 1])
        w3c = sb("w3c", [P, M2])
        k3 = sb("k3", [P, 1])
        kc = sb("kc", [P, 1])
        st1 = sb("st1", [P, K2, TILES, 6])
        st2 = sb("st2", [P, M2, TILES, 6])
        mv1 = sb("mv1", [P, K2, 2])
        mv2 = sb("mv2", [P, M2, 2])
        ve = sb("ve", [P, K2])
        sd = sb("sd", [P, K2])
        r0 = sb("r0", [P, K2])
        nt = sb("nt", [P, K2])
        a1 = sb("a1", [P, K2])
        c1 = sb("c1", [P, K2])
        b2f = sb("b2f", [P, M2])
        a2 = sb("a2", [P, M2])
        v2 = sb("v2", [P, M2])
        s2 = sb("s2", [P, M2])
        s2s = sb("s2s", [P, 1])
        y_pair = sb("y_pair", [P, COLS])
        y_sb = sb("y_sb", [P, COLS])

        ps = [ctx.enter_context(nc.psum_tensor(f"ps{i}", [P, NT], FP32)) for i in range(8)]
        ps_y, ps_m = ps[6], ps[7]
        ps_par = ps_m[:, 0:NPAR]
        ps_b2 = ps_m[:, 64:64 + M2]
        ps_k = ps_m[:, 96:97]

        x_loaded = sem("x_loaded")
        w_loaded = [sem(f"w_loaded{i}") for i in range(W_STAGE)]
        w2b_loaded = sem("w2b_loaded")
        c_loaded = sem("c_loaded")
        par_loaded = sem("par_loaded")
        l3_loaded = sem("l3_loaded")
        y_stored = sem("y_stored")
        pool_set = sem("pool_set")
        par_turned = sem("par_turned")
        par_ready = sem("par_ready")
        c_split = sem("c_split")
        c_built = sem("c_built")
        turned = sem("turned")
        x_hi = sem("x_hi")
        x_lo = sem("x_lo")
        w_hi = sem("w_hi")
        w_lo = sem("w_lo")
        pe_steps = sem("pe_steps")
        m_done = sem("m_done")
        prod_done = sem("prod_done")
        sum_done = sem("sum_done")
        h1_ready = sem("h1_ready")
        st1_done = sem("st1_done")
        yp_done = sem("yp_done")
        yp_saved = sem("yp_saved")
        ve_ready = sem("ve_ready")
        sd_ready = sem("sd_ready")
        a1_ready = sem("a1_ready")
        w2_hi = sem("w2_hi")
        w2_lo = sem("w2_lo")
        h_hi = sem("h_hi")
        h_lo = sem("h_lo")
        pe_steps2 = sem("pe_steps2")
        b2_done = sem("b2_done")
        b2_ready = sem("b2_ready")
        m2_done = sem("m2_done")
        h2_ready = sem("h2_ready")
        v2_ready = sem("v2_ready")
        s2_ready = sem("s2_ready")
        y_done = sem("y_done")
        y_ready = sem("y_ready")
        dve_chain = sem("dve_chain")

        x_v = x.rearrange("(n j g) i d -> n j g (i d)", n=TILES, j=32)
        w1_v = W1.rearrange("(i t e) n -> t i e n", t=KT, e=DK)
        steps = TILES * KT
        VE = [K2 // 2, K2 // 2, M2 - 1, 1]

        def turned_slot(s, k):
            if s == 0 and k >= XT_SLOTS:
                return h1[:, MT + (k - XT_SLOTS) // TILES, (k - XT_SLOTS) % TILES, :]
            return xT[:, k % XT_SLOTS, :]

        def load_x(eng, n, quarters):
            for q in quarters:
                eng.dma_start(x_raw[32 * q:32 * q + 32, :, :],
                              x_v[n, :, :, q * NT:(q + 1) * NT]).then_inc(x_loaded, 16)

        def reload_x(eng, u, n, quarters):
            eng.wait_ge(turned, u * KT)
            load_x(eng, n, quarters)

        def by_rows(tile):
            return tile.rearrange("p (g j) -> p g j", j=32)

        block = ctx.enter_context(nc.Block())

        @block.sync
        def _(sp):
            def load_w1(s, k):
                if s or k >= W_STAGE:
                    sp.wait_ge(w_hi, s * KT + k - W_STAGE + 1)
                    sp.wait_ge(w_lo, s * KT + k - W_STAGE + 1)
                sp.dma_start(w_raw[:, k % W_STAGE, :],
                             w1_v[k, :, :, s * HALF:(s + 1) * HALF]).then_inc(w_loaded[k % W_STAGE], 16)

            for s in range(2):
                if s == 0:
                    load_x(sp, 0, (0, 1))
                for k in range(KT):
                    load_w1(s, k)
                    if k == TURNED_EARLY + W_STAGE:
                        reload_x(sp, s * TILES + 1, 1, (0, 1))
                with sp.Fori(2, TILES) as n:
                    reload_x(sp, n + s * TILES, n, (0, 1))
                if s == 0:
                    reload_x(sp, TILES, 0, (0, 1))
            for k in range(K2 // 2):
                sp.wait_ge(w_hi, KT + KT - W_STAGE + k + 1)
                sp.wait_ge(w_lo, KT + KT - W_STAGE + k + 1)
                sp.dma_start(w_raw[:, k, :], W2[k * P:(k + 1) * P, :]).then_inc(w_loaded[k], 16)
            sp.wait_ge(x_hi, 2 * steps)
            sp.wait_ge(x_lo, 2 * steps)
            sp.dma_start(xT[:, 0:K2 // 2, :],
                         W2[H1 // 2:H1, :].rearrange("(k p) n -> p k n", p=P)).then_inc(w2b_loaded, 16)
            sp.wait_ge(y_ready, 1)
            sp.dma_start(out.rearrange("(p c) o -> p (c o)", c=COLS), y_sb[:, :]).then_inc(y_stored, 16)
            sp.wait_ge(y_stored, 16)

        @block.gpsimd
        def _(pool):
            pool.memset(c_raw[:, :], 0.0).then_inc(pool_set, 1)
            pool.memset(ident[:, :], 0.0).then_inc(pool_set, 1)
            pool.memset(ones[:, :], 1.0).then_inc(pool_set, 1)
            pool.wait_ge(pool_set, 3)
            pool.affine_select(out=ident[:, :], in_=ident[:, :], compare_op=ALU.not_equal, fill=1.0, base=0,
                               pattern=[[-1, P]], channel_multiplier=1).then_inc(pool_set, 1)
            for s in range(2):
                for k in range(KT):
                    pool.wait_ge(w_loaded[k % W_STAGE], 16 * (s * KT // W_STAGE + k // W_STAGE + 1))
                    pool.wait_ge(w_hi, s * KT + k + 1)
                    if s:
                        pool.wait_ge(pe_steps, steps - KT + k + 1)
                    pool.tensor_tensor(w_hl[:, k, 1, :], w_raw[:, k % W_STAGE, :],
                                       w_hl[:, k, 0, :].bitcast(FP32), ALU.subtract).then_inc(w_lo, 1)

        @block.scalar
        def _(act):
            load_x(act, 0, (2, 3))
            act.wait_ge(pool_set, 1)
            for i in range(NF - 1):
                at = HO + i * (2 * NF - i - 1) // 2
                src = Wc[at:at + NF - 1 - i, :].rearrange("a o -> o a").to_broadcast([DK, NF - 1 - i])
                act.dma_start(c_raw[DK * i:DK * i + DK, i + 1:NF], src).then_inc(c_loaded, 16)
            for i, v in enumerate((b1, g1, beta1)):
                act.dma_start(par_rows[i * K2:(i + 1) * K2, :],
                              v.rearrange("(m p) -> m p", p=P)).then_inc(par_loaded, 16)
            for i, v in enumerate((b2, g2, beta2)):
                act.dma_start(par_rows[3 * K2 + i * M2:3 * K2 + (i + 1) * M2, :],
                              v.rearrange("(m p) -> m p", p=P)).then_inc(par_loaded, 16)
            act.dma_start(w3[:, :, :], W3.rearrange("(m p) h -> p m h", p=P)).then_inc(l3_loaded, 16)
            act.dma_start(wc_b[:, :], Wc[0:HO, :].rearrange("a o -> o a").to_broadcast([P, HO])).then_inc(l3_loaded, 16)
            act.dma_start(b3_b[:, :], b3.rearrange("(o a) -> o a", o=1).to_broadcast([P, HO])).then_inc(l3_loaded, 16)
            act.dma_start(bc_b[:, :], bc.rearrange("(o a) -> o a", o=1).to_broadcast([P, 1])).then_inc(l3_loaded, 16)
            def hi_of_w1(s, k):
                act.wait_ge(w_loaded[k % W_STAGE], 16 * (s * KT // W_STAGE + k // W_STAGE + 1))
                if s:
                    act.wait_ge(pe_steps, steps - KT + k + 1)
                act.copy(w_hl[:, k, 0, :], w_raw[:, k % W_STAGE, :]).then_inc(w_hi, 1)

            def hi_of_x(s, u, k, n_next, first=False):
                act.wait_ge(turned, u * KT + k + 1)
                if not (first and k < HL_SLOTS):
                    act.wait_ge(pe_steps, u * KT + k - HL_SLOTS + 1)
                act.copy(x_hl[:, k % HL_SLOTS, 0, :], turned_slot(s, k)).then_inc(x_hi, 1)
                if k == TURNED_EARLY + 1 and n_next is not None:
                    reload_x(act, u + 1, n_next, (2, 3))

            def relu1(s, u, n):
                for m in range(MT):
                    if m < MT - 1:
                        act.wait_ge(m_done, (u - 1) * (MT - 1) + m + 1)
                    else:
                        act.wait_ge(pe_steps, u * KT)
                    act.activation(h1[:, s * MT + m, n, :], ps[m][:, :], ACT.Relu,
                                   bias=b1_c[:, s * MT + m:s * MT + m + 1]).then_inc(h1_ready, 1)

            def tile1(s, u, n, n_next):
                for k in range(KT):
                    if k == HL_SLOTS - 1:
                        relu1(s, u, n - 1)
                    hi_of_x(s, u, k, n_next)

            for s in range(2):
                for k in range(KT):
                    if s and k == HL_SLOTS - 1:
                        relu1(0, TILES, TILES - 1)
                    hi_of_w1(s, k)
                    hi_of_x(s, s * TILES, k, 1, first=(s == 0))
                    if s == 0 and k == 0:
                        act.wait_ge(c_built, 1)
                        act.copy(c_hl[:, 0, :], c_full[:, :, :].rearrange("p j e -> p (j e)")).then_inc(c_split, 1)
                if s == 0:
                    act.wait_ge(par_ready, 1)
                else:
                    act.wait_ge(yp_saved, 1)
                with act.Fori(1, TILES - 1) as n:
                    tile1(s, n + s * TILES, n, n + 1)
                tile1(s, (s + 1) * TILES - 1, TILES - 1, None if s else 0)

            def root(n):
                act.wait_ge(ve_ready, n + 1)
                act.activation(sd[:, 0:VE[n]], ve[:, 0:VE[n]], ACT.Sqrt).then_inc(sd_ready, 1)

            def hi_of_w2(k):
                act.wait_ge(a1_ready, 1 + k // (K2 // 2))
                if k < K2 // 2:
                    act.wait_ge(w_loaded[k], 16 * (2 * KT // W_STAGE + 1))
                    act.wait_ge(pe_steps, 2 * steps - KT + K2)
                    src = w_raw[:, k, :]
                else:
                    act.wait_ge(w2b_loaded, 16)
                    src = xT[:, k - K2 // 2, :]
                act.activation(w_hl[:, k, 0, :], src, ACT.Copy, scale=a1[:, k:k + 1]).then_inc(w2_hi, 1)

            def hi_of_h1(n, k, first):
                if first:
                    act.wait_ge(pe_steps, 2 * steps - KT + K2 + k + 1)
                    if k >= K2 // 2:
                        act.wait_ge(h1_ready, 2 * TILES * MT)
                else:
                    act.wait_ge(pe_steps2, (n - 1) * K2 + k + 1)
                act.copy(w_hl[:, K2 + k, 0, :], h1[:, k, n, :]).then_inc(h_hi, 1)

            def relu2(n):
                for m in range(M2):
                    if m < M2 - 1:
                        act.wait_ge(m2_done, n * (M2 - 1) + m + 1)
                    else:
                        act.wait_ge(pe_steps2, (n + 1) * K2)
                    act.activation(h2[:, m, :, n, :], by_rows(ps[m][:, :]), ACT.Relu, bias=b2f[:, m:m + 1]).then_inc(h2_ready, 1)

            root(0)
            for k in range(K2 // 2):
                hi_of_w2(k)
            for k in range(K2 // 2):
                hi_of_h1(0, k, True)
            relu1(1, 2 * TILES, TILES - 1)
            for k in range(K2 // 2, K2):
                hi_of_h1(0, k, True)
            root(1)
            for k in range(K2 // 2, K2):
                hi_of_w2(k)
            act.wait_ge(b2_ready, 1)
            with act.Fori(1, TILES) as n:
                for k in range(K2):
                    if k == K2 - 1:
                        relu2(n - 1)
                    hi_of_h1(n, k, False)
            for m in range(M2):
                act.wait_ge(m2_done, (TILES - 1) * (M2 - 1) + m + 1)
                act.activation(h2[:, m, :, TILES - 1, :], by_rows(ps[m][:, :]), ACT.Relu, bias=b2f[:, m:m + 1]).then_inc(h2_ready, 1)
                if m >= M2 - 2:
                    root(m - M2 + 4)

        @block.tensor
        def _(pe):
            pe.wait_ge(pool_set, 4)
            pe.wait_ge(par_loaded, 96)
            pe.transpose(ps_par, par_rows[:, :], ident[0:NPAR, 0:NPAR]).then_inc(par_turned, 1)

            def three(acc, w_hi_ap, w_lo_ap, x_hi_ap, x_lo_ap, start, stop):
                pe.matmul(acc, w_hi_ap, x_hi_ap, start=start, stop=False)
                pe.matmul(acc, w_hi_ap, x_lo_ap, start=False, stop=False)
                return pe.matmul(acc, w_lo_ap, x_hi_ap, start=False, stop=stop)

            def step1(s, u, k, first_in_sweep):
                hi, lo = x_hl[:, k % HL_SLOTS, 0, :], x_hl[:, k % HL_SLOTS, 1, :]
                pe.wait_ge(x_hi, u * KT + k + 1)
                pe.wait_ge(x_lo, u * KT + k + 1)
                if first_in_sweep:
                    pe.wait_ge(w_hi, s * KT + k + 1)
                    pe.wait_ge(w_lo, s * KT + k + 1)
                for m in range(MT):
                    if k == 0 and not (s == 0 and first_in_sweep):
                        pe.wait_ge(h1_ready, (u - 1) * MT + m + 1)
                    cols = slice(m * P, (m + 1) * P)
                    mm = three(ps[m][:, :], w_hl[:, k, 0, cols], w_hl[:, k, 1, cols], hi, lo, k == 0, k == KT - 1)
                    if k == KT - 1 and m < MT - 1:
                        mm.then_inc(m_done, 1)
                if s == 0:
                    if first_in_sweep and k == 0:
                        pe.wait_ge(c_split, 2)
                    if not (first_in_sweep and k < 2):
                        pe.wait_ge(prod_done, u * KT + k - 1)
                    mm = three(ps[4 + k % 2][:, :], c_hl[:, 0, :], c_hl[:, 1, :], hi, lo, True, True)
                mm.then_inc(pe_steps, 1)

            for s in range(2):
                for k in range(KT):
                    step1(s, s * TILES, k, True)
                    if s and k == 7:
                        pe.wait_ge(sum_done, TILES * (KT - 1))
                        for c in range(COLS):
                            mm = pe.matmul(ps_y[:, c:c + 1], pair_sum[:, c, :, :].rearrange("p n j -> p (n j)"),
                                           ones[:, 0:1], start=True, stop=True)
                        mm.then_inc(yp_done, 1)
                with pe.Fori(1, TILES) as n:
                    for k in range(KT):
                        step1(s, n + s * TILES, k, False)

            def step2(n, k, first, m_from=0, m_to=M2):
                pe.wait_ge(h_hi, n * K2 + k + 1)
                pe.wait_ge(h_lo, n * K2 + k + 1)
                if first:
                    pe.wait_ge(w2_hi, k + 1)
                    pe.wait_ge(w2_lo, k + 1)
                for m in range(m_from, m_to):
                    if k == 0:
                        if first:
                            pe.wait_ge(h1_ready, (2 * TILES - 1) * MT + m + 1)
                        else:
                            pe.wait_ge(h2_ready, (n - 1) * M2 + m + 1)
                    cols = slice(m * P, (m + 1) * P)
                    mm = three(ps[m][:, :], w_hl[:, k, 0, cols], w_hl[:, k, 1, cols],
                               w_hl[:, K2 + k, 0, :], w_hl[:, K2 + k, 1, :], k == 0, k == K2 - 1)
                    if k == K2 - 1 and (m < M2 - 1 or m_from):
                        mm.then_inc(m2_done, 1)
                    elif m == M2 - 1 and not m_from:
                        mm.then_inc(pe_steps2, 1)

            for k in range(K2):
                step2(0, k, True)
                if k == K2 // 2:
                    pe.wait_ge(a1_ready, 2)
                    for m in range(M2):
                        for kk in range(K2):
                            w = w_raw[:, kk, m * P:(m + 1) * P] if kk < K2 // 2 else \
                                xT[:, kk - K2 // 2, m * P:(m + 1) * P]
                            mm = pe.matmul(ps_b2[:, m:m + 1], w, c1[:, kk:kk + 1], start=(kk == 0), stop=(kk == K2 - 1))
                    mm.then_inc(b2_done, 1)
            with pe.Fori(1, TILES - 1) as n:
                for k in range(K2):
                    step2(n, k, False)
            for m in range(M2):
                for k in range(K2):
                    step2(TILES - 1, k, False, m, m + 1)
            pe.wait_ge(yp_saved, 1)
            for m in range(M2):
                pe.wait_ge(v2_ready, 1 if m < M2 - 1 else 2)
                for c in range(COLS):
                    mm = pe.matmul(ps_y[:, c:c + 1], h2[:, m, c, :, :].rearrange("p n j -> p (n j)"), v2[:, m:m + 1],
                                   start=(m == 0 and c == 0), stop=(m == M2 - 1), skip_group_check=True)
            mm.then_inc(y_done, 1)
            pe.wait_ge(s2_ready, 1)
            pe.matmul(ps_k, ones[:, :], s2s[:, :], start=True, stop=True).then_inc(y_done, 1)

        @block.vector
        def _(dve):
            chain = [0]

            def link(ins):
                chain[0] += 1
                ins.then_inc(dve_chain, 1)
                dve.wait_ge(dve_chain, chain[0])

            def build_c():
                dve.wait_ge(pool_set, 4)
                link(dve.tensor_reduce(c_mask[:, :], ident[:, :].rearrange("p (i e) -> p e i", e=DK), AX.X, ALU.max))
                dve.wait_ge(c_loaded, 16 * (NF - 1))
                for e in range(DK):
                    last = dve.tensor_scalar(c_full[:, :, e], c_raw[:, :], c_mask[:, e:e + 1], None, ALU.mult)
                last.then_inc(c_built, 1)
                dve.wait_ge(c_split, 1)
                dve.tensor_tensor(c_hl[:, 1, :], c_full[:, :, :].rearrange("p j e -> p (j e)"),
                                  c_hl[:, 0, :].bitcast(FP32), ALU.subtract).then_inc(c_split, 1)

            def turn(s, u, k, first=False, after_a=False):
                if s == 1 and k >= XT_SLOTS:
                    dve.wait_ge(x_lo, u * KT + k - XT_SLOTS + 1)
                elif not first:
                    dve.wait_ge(x_lo, (u - 1) * KT + (k + XT_SLOTS if s == 1 and not after_a else k) + 1)
                    if s == 0 or after_a:
                        dve.wait_ge(prod_done, (u - 1) * KT + k + 1)
                if k == 0:
                    dve.wait_ge(x_loaded, (u + 1) * 64)
                dve.transpose(turned_slot(s, k),
                              x_raw[:, :, :].rearrange("p b (i d) -> p b i d", d=D)[:, :, :, DK * k:DK * k + DK]
                              ).then_inc(turned, 1)

            def lo_of_x(s, u, k, first=False):
                dve.wait_ge(x_hi, u * KT + k + 1)
                if not (first and k < HL_SLOTS):
                    dve.wait_ge(pe_steps, u * KT + k - HL_SLOTS + 1)
                dve.tensor_tensor(x_hl[:, k % HL_SLOTS, 1, :], turned_slot(s, k),
                                  x_hl[:, k % HL_SLOTS, 0, :].bitcast(FP32), ALU.subtract).then_inc(x_lo, 1)

            def product(n, k):
                dve.wait_ge(pe_steps, n * KT + k + 1)
                dst = pair_sum[:, :, n, :] if k == 0 else by_rows(pair_prod[:, k % 4, :])
                dve.tensor_tensor(dst, by_rows(ps[4 + k % 2][:, :]), by_rows(turned_slot(0, k)),
                                  ALU.mult).then_inc(prod_done, 1)

            def add_up(n, k):
                dve.wait_ge(prod_done, n * KT + k + 1)
                if k >= 2:
                    dve.wait_ge(sum_done, n * (KT - 1) + k - 1)
                dve.tensor_tensor(pair_sum[:, :, n, :], pair_sum[:, :, n, :], by_rows(pair_prod[:, k % 4, :]),
                                  ALU.add).then_inc(sum_done, 1)

            def stats1(s, u, n, m):
                dve.wait_ge(h1_ready, (u - 1) * MT + m + 1)
                dve.bn_stats(st1[:, s * MT + m, n, :], h1[:, s * MT + m, n, :]).then_inc(st1_done, 1)

            def steps_of(s, u, n, first=False, last=False):
                for k in range(KT):
                    if k < LAG and (s == 0 and not first or s == 1 and first):
                        product(n - 1, KT + k - LAG)
                    elif k >= LAG and s == 0:
                        product(n, k - LAG)
                    lo_of_x(s, u, k, first and s == 0)
                    for kk in (2 * k + 1, 2 * k + 2):
                        if kk < KT:
                            turn(s, u, kk, first and s == 0, first and s == 1)
                    if k == KT - 1 and not last:
                        turn(s, u + 1, 0)
                    if k <= LAG and (s == 0 and not first or s == 1 and first):
                        add_up(n - 1, KT + k - LAG - 1)
                    elif k >= LAG + 2 and s == 0:
                        add_up(n, k - LAG - 1)
                    if HL_SLOTS <= k < HL_SLOTS + MT:
                        if not first:
                            stats1(s, u, n - 1, k - HL_SLOTS)
                        elif s:
                            stats1(s - 1, u, TILES - 1, k - HL_SLOTS)
                    if first and s == 0 and k == 0:
                        build_c()

            def fold_scale(g, be, mv, a, c, lo, hi, batch):
                w = hi - lo
                dve.tensor_scalar(ve[:, 0:w], mv[:, lo:hi, 1], EPS, None, ALU.add).then_inc(ve_ready, 1)
                dve.wait_ge(sd_ready, batch + 1)
                link(dve.reciprocal(r0[:, 0:w], sd[:, 0:w]))
                link(dve.tensor_tensor(nt[:, 0:w], r0[:, 0:w], r0[:, 0:w], ALU.mult))
                link(dve.tensor_tensor(nt[:, 0:w], nt[:, 0:w], ve[:, 0:w], ALU.mult))
                link(dve.tensor_scalar(nt[:, 0:w], nt[:, 0:w], -0.5, 1.5, ALU.mult, ALU.add))
                link(dve.tensor_tensor(nt[:, 0:w], nt[:, 0:w], r0[:, 0:w], ALU.mult))
                link(dve.tensor_tensor(a[:, lo:hi], nt[:, 0:w], g[:, lo:hi], ALU.mult))
                link(dve.tensor_tensor(nt[:, 0:w], mv[:, lo:hi, 0], a[:, lo:hi], ALU.mult))
                return dve.tensor_tensor(c[:, lo:hi], be[:, lo:hi], nt[:, 0:w], ALU.subtract)

            def lo_of_w2(k):
                dve.wait_ge(w2_hi, k + 1)
                src = w_raw[:, k, :] if k < K2 // 2 else xT[:, k - K2 // 2, :]
                dve.scalar_tensor_tensor(w_hl[:, k, 1, :], src, a1[:, k:k + 1], w_hl[:, k, 0, :].bitcast(FP32),
                                         ALU.mult, ALU.subtract).then_inc(w2_lo, 1)

            def lo_of_h1(n, k):
                dve.wait_ge(h_hi, n * K2 + k + 1)
                dve.tensor_tensor(w_hl[:, K2 + k, 1, :], h1[:, k, n, :], w_hl[:, K2 + k, 0, :].bitcast(FP32),
                                  ALU.subtract).then_inc(h_lo, 1)

            for s in range(2):
                if s == 0:
                    turn(0, 0, 0, first=True)
                steps_of(s, s * TILES, s * TILES, first=True)
                if s == 0:
                    dve.wait_ge(par_turned, 1)
                    dve.tensor_copy(par[:, :], ps_par).then_inc(par_ready, 1)
                    dve.wait_ge(l3_loaded, 64)
                    for m in range(M2):
                        link(dve.tensor_tensor(w3p[:, :], w3[:, m, :], wc_b[:, :], ALU.mult))
                        link(dve.tensor_reduce(w3c[:, m:m + 1], w3p[:, :], AX.X, ALU.add))
                    link(dve.tensor_tensor(w3p[:, :], b3_b[:, :], wc_b[:, :], ALU.mult))
                    link(dve.tensor_reduce(k3[:, :], w3p[:, :], AX.X, ALU.add))
                    link(dve.tensor_tensor(k3[:, :], k3[:, :], bc_b[:, :], ALU.add))
                else:
                    dve.wait_ge(yp_done, 1)
                    dve.tensor_copy(y_pair[:, :], ps_y[:, 0:COLS]).then_inc(yp_saved, 1)
                with dve.Fori(1, TILES - s) as n:
                    steps_of(s, n + s * TILES, n)
            steps_of(1, 2 * TILES - 1, TILES - 1, last=True)

            dve.wait_ge(st1_done, TILES * MT)
            for m in range(MT):
                link(dve.bn_aggr(mv1[:, m, :], st1[:, m, :, :].rearrange("p t s -> p (t s)")))
            fold_scale(g1_c, be1_c, mv1, a1, c1, 0, MT, 0).then_inc(a1_ready, 1)
            for k in range(K2 // 2):
                lo_of_w2(k)
            for k in range(K2 // 2):
                lo_of_h1(0, k)
            for m in range(MT):
                stats1(1, 2 * TILES, TILES - 1, m)
            dve.wait_ge(st1_done, 2 * TILES * MT)
            for m in range(MT, K2):
                link(dve.bn_aggr(mv1[:, m, :], st1[:, m, :, :].rearrange("p t s -> p (t s)")))
            fold_scale(g1_c, be1_c, mv1, a1, c1, MT, K2, 1).then_inc(a1_ready, 1)
            for k in range(K2 // 2, K2):
                lo_of_w2(k)
                lo_of_h1(0, k)
            dve.wait_ge(b2_done, 1)
            dve.tensor_tensor(b2f[:, :], ps_b2, b2_c, ALU.add).then_inc(b2_ready, 1)

            def stats2(n, m):
                dve.wait_ge(h2_ready, n * M2 + m + 1)
                return dve.bn_stats(st2[:, m, n, :], h2[:, m, :, n, :])

            with dve.Fori(1, TILES) as n:
                for k in range(K2 - 1):
                    lo_of_h1(n, k)
                for m in range(M2):
                    stats2(n - 1, m)
                lo_of_h1(n, K2 - 1)

            def norm2(lo, hi, batch):
                for m in range(lo, hi):
                    link(stats2(TILES - 1, m))
                    link(dve.bn_aggr(mv2[:, m, :], st2[:, m, :, :].rearrange("p t s -> p (t s)")))
                link(fold_scale(g2_c, be2_c, mv2, a2, s2, lo, hi, batch))
                dve.tensor_tensor(v2[:, lo:hi], a2[:, lo:hi], w3c[:, lo:hi], ALU.mult).then_inc(v2_ready, 1)
                link(dve.tensor_tensor(s2[:, lo:hi], s2[:, lo:hi], w3c[:, lo:hi], ALU.mult))

            norm2(0, M2 - 1, 2)
            norm2(M2 - 1, M2, 3)
            dve.tensor_reduce(s2s[:, :], s2[:, :], AX.X, ALU.add).then_inc(s2_ready, 1)
            dve.wait_ge(y_done, 2)
            link(dve.tensor_tensor(kc[:, :], k3[:, :], ps_k, ALU.add))
            dve.scalar_tensor_tensor(y_sb[:, :], ps_y[:, 0:COLS], kc[:, 0:1], y_pair[:, :], ALU.add,
                                     ALU.add).then_inc(y_ready, 1)


_INS = ['r_x', 'L0_rec_W1', 'L0_rec_b1', 'L0_rec_g1', 'L0_rec_beta1', 'L0_rec_W2', 'L0_rec_b2', 'L0_rec_g2',
        'L0_rec_beta2', 'L0_rec_W3', 'L0_rec_b3', 'L0_rec_Wc', 'L0_rec_bc']
_OUTS = [((B, 1), 'float32')]


def kernel(**inputs):
    import numpy as _np
    import concourse.bacc as _bacc
    from concourse import mybir as _mybir
    from concourse.bass_utils import run_bass_kernel_spmd as _run

    nc = _bacc.Bacc("TRN2", target_bir_lowering=False, num_devices=1)
    arrays, args = {}, []
    for name in _INS:
        a = _np.ascontiguousarray(inputs[name])
        arrays[f"in_{name}_dram"] = a
        args.append(nc.dram_tensor(f"in_{name}_dram", a.shape, _mybir.dt.from_np(a.dtype), kind="ExternalInput").ap())
    for i, (shape, dtype) in enumerate(_OUTS):
        dt = _mybir.dt.from_np(_np.dtype(dtype))
        args.append(nc.dram_tensor(f"out_{i}_dram", shape, dt, kind="ExternalOutput").ap())
    build(nc, *args)
    r = _run(nc, [arrays], core_ids=[0])
    got = tuple(r.results[0][f"out_{i}_dram"] for i in range(len(_OUTS)))
    return got[0]
```

```python
import concourse.bass as bass
from concourse import mybir
from contextlib import ExitStack

FP32 = mybir.dt.float32
FP32R = mybir.dt.float32r
ALU = mybir.AluOpType
ACT = mybir.ActivationFunctionType
AX = mybir.AxisListType

P = 128
B, NF, D = 2048, 32, 64
F = NF * D
H1, H2, HO = 1024, 512, 64
EPS = 1e-5
NT = 512
TILES = B // NT
KT = F // P
DK = P // NF
HALF = H1 // 2
MT = HALF // P
K2 = H1 // P
M2 = H2 // P
XT_SLOTS = 8
HL_SLOTS = 4
W_STAGE = 4
PROD = 2
BLKS = NT // 32
HB = NT // 2
HALVES = (slice(0, BLKS // 2), slice(BLKS // 2, BLKS))
V_B = TILES + 1
V_END = V_B + TILES
LAG = HL_SLOTS
WARM_UP = 22
HALF1_AT = 3 * KT // 4
C_AT = KT - 6
TURN_HALF = 3
TURNED_EARLY = KT // 2


def build(nc, x, W1, b1, g1, beta1, W2, b2, g2, beta2, W3, b3, Wc, bc, out):
    ctx = ExitStack()
    with ctx:
        def sb(name, shape, dt=FP32):
            return ctx.enter_context(nc.sbuf_tensor(name, shape, dt))

        def sem(name):
            return ctx.enter_context(nc.semaphore(name))

        w_hl = sb("w_hl", [P, KT, 2, HALF], FP32R)
        x_hl = sb("x_hl", [P, HL_SLOTS, 2, NT], FP32R)
        xT = sb("xT", [P, XT_SLOTS, NT])
        x_raw = sb("x_raw", [P, BLKS, NT])
        h1 = sb("h1", [P, K2, TILES, NT])
        sum_in = sb("sum_in", [P, TILES, NT])
        pair_prod = sb("pair_prod", [P, PROD, NT])
        h2 = x_raw[:, :, :].rearrange("p (m n) c -> p m n c", m=M2)
        c1w2 = x_raw[:, 0, :]
        w2_raw = x_raw[:, 1:1 + K2, :]
        setup = h1[:, K2 - 2, :, :]
        ident = setup[:, 0, 0:P]
        c_full = setup[:, 0, P:2 * P].rearrange("p (j e) -> p j e", e=DK)
        ones = sb("ones", [P, P])
        c_raw = sb("c_raw", [P, NF])
        c_mask = sb("c_mask", [P, DK])
        c_hl = sb("c_hl", [P, 2, P], FP32R)
        NPAR = 3 * K2 + 3 * M2
        par_rows = setup[0:NPAR, 1, 0:P]
        par = sb("par", [P, NPAR])
        b1_c, g1_c, be1_c = (par[:, i * K2:(i + 1) * K2] for i in range(3))
        b2_c, g2_c, be2_c = (par[:, 3 * K2 + i * M2:3 * K2 + (i + 1) * M2] for i in range(3))
        w3 = xT[:, 0, 0:M2 * HO].rearrange("p (m h) -> p m h", m=M2)
        w3p = xT[:, 1, 0:M2 * HO].rearrange("p (m h) -> p m h", m=M2)
        wc_b, b3_b, b3p = (xT[:, 2, i * HO:(i + 1) * HO] for i in range(3))
        y_sb = xT[0:1, XT_SLOTS - TILES:, :]
        bc_b = sb("bc_b", [P, 1])
        w3c = sb("w3c", [P, M2])
        gw = sb("gw", [P, M2])
        bw = sb("bw", [P, M2])
        warm = sb("warm", [P, 1])
        k3 = sb("k3", [P, 1])
        kc = sb("kc", [P, 1])
        st1 = sb("st1", [P, K2, TILES, 6])
        st2 = sb("st2", [P, M2, TILES, 6])
        mv1 = sb("mv1", [P, K2, 2])
        mv2 = sb("mv2", [P, M2, 2])
        ve = sb("ve", [P, K2])
        sd = sb("sd", [P, K2])
        r0 = sb("r0", [P, K2])
        nt = sb("nt", [P, K2])
        a1 = sb("a1", [P, K2])
        c1 = sb("c1", [P, K2])
        b2f = sb("b2f", [P, M2])
        v2 = sb("v2", [P, M2])
        s2 = sb("s2", [P, M2])
        s2s = sb("s2s", [P, 1])

        ps = [ctx.enter_context(nc.psum_tensor(f"ps{i}", [P, NT], FP32)) for i in range(8)]
        ps_par = ps[7][:, 0:NPAR]
        ps_c = ps[6][:, 0:P]
        ps_sum = ps[6][:, :]
        ps_b2 = ps[7][:, 64:64 + M2]
        ps_y = [ps[4 + n][0:1, :] for n in range(TILES)]
        ps_k = ps[0][0:1, 0:1]

        x_first = sem("x_first")
        x_loaded = sem("x_loaded")
        w_loaded = [sem(f"w_loaded{k}") for k in range(KT)]
        w2_loaded = sem("w2_loaded")
        c_loaded = sem("c_loaded")
        par_loaded = sem("par_loaded")
        l3_loaded = sem("l3_loaded")
        y_stored = sem("y_stored")
        pool_set = sem("pool_set")
        par_turned = sem("par_turned")
        par_ready = sem("par_ready")
        c_split = sem("c_split")
        c_built = sem("c_built")
        c_turned = sem("c_turned")
        x_plus = sem("x_plus")
        turned = sem("turned")
        x_hi = sem("x_hi")
        x_lo = sem("x_lo")
        w_hi = sem("w_hi")
        w_lo = sem("w_lo")
        pe_steps = sem("pe_steps")
        m_done = sem("m_done")
        prod_done = sem("prod_done")
        sum_done = sem("sum_done")
        h1_ready = sem("h1_ready")
        st1_done = sem("st1_done")
        ve_ready = sem("ve_ready")
        sd_ready = sem("sd_ready")
        a1_ready = sem("a1_ready")
        w2_hi = sem("w2_hi")
        w2_lo = sem("w2_lo")
        c1w2_added = sem("c1w2_added")
        h_hi = sem("h_hi")
        h_lo = sem("h_lo")
        pe_steps2 = sem("pe_steps2")
        b2_done = sem("b2_done")
        b2_ready = sem("b2_ready")
        m2_done = sem("m2_done")
        h2_ready = sem("h2_ready")
        h2_added = sem("h2_added")
        v2_ready = sem("v2_ready")
        s2_ready = sem("s2_ready")
        k_done = sem("k_done")
        kc_ready = sem("kc_ready")
        y_done = sem("y_done")
        y_ready = sem("y_ready")
        dve_chain = sem("dve_chain")

        x_v = x.rearrange("(n j g) i d -> n j g (i d)", n=TILES, j=32)
        w1_v = W1.rearrange("(i t e) n -> t i e n", t=KT, e=DK)
        VE = [K2 // 2, K2 // 2] + [1] * M2
        AT_W2 = list(range(TURNED_EARLY + 1, KT, 2))

        def turned_slot(many, k):
            if many and k >= XT_SLOTS:
                return h1[:, MT + (k - XT_SLOTS) // TILES, (k - XT_SLOTS) % TILES, :]
            return xT[:, k % XT_SLOTS, :]

        def w_stage(s, k):
            return h1[:, k // TILES, k % TILES, :] if s == 0 else h1[:, K2 - 2, k % W_STAGE, :]

        def load_x(eng, n, quarters, done, groups=slice(0, BLKS)):
            for q in quarters:
                eng.dma_start(x_raw[32 * q:32 * q + 32, groups, :],
                              x_v[n, :, groups, q * NT:(q + 1) * NT]).then_inc(done, 16)

        def reload_x(eng, v, n, quarters, done=x_loaded, groups=slice(0, BLKS)):
            eng.wait_ge(turned, v * KT)
            load_x(eng, n, quarters, done, groups)

        def row(tiles):
            return tiles.rearrange("p n c -> p (n c)")

        def by_rows(tile):
            return tile.rearrange("p (g j) -> p g j", j=32)

        block = ctx.enter_context(nc.Block())

        @block.sync
        def _(sp):
            def load_w1(s, k):
                if s:
                    sp.wait_ge(w_hi, KT + max(k - W_STAGE + 1, 0))
                    sp.wait_ge(w_lo, KT + max(k - W_STAGE + 1, 0))
                sp.dma_start(w_stage(s, k), w1_v[k, :, :, s * HALF:(s + 1) * HALF]).then_inc(w_loaded[k], 16)

            load_w1(0, 0)
            load_x(sp, 0, (0, 1), x_first, HALVES[0])
            for k in range(1, HALF1_AT):
                load_w1(0, k)
            load_x(sp, 0, (0, 1), x_loaded, HALVES[1])
            for k in range(HALF1_AT, KT):
                load_w1(0, k)
            for i, v in enumerate((b1, g1, beta1)):
                sp.dma_start(par_rows[i * K2:(i + 1) * K2, :],
                             v.rearrange("(m p) -> m p", p=P)).then_inc(par_loaded, 16)
            for i, v in enumerate((b2, g2, beta2)):
                sp.dma_start(par_rows[3 * K2 + i * M2:3 * K2 + (i + 1) * M2, :],
                             v.rearrange("(m p) -> m p", p=P)).then_inc(par_loaded, 16)
            sp.wait_ge(pool_set, 1)
            for i in range(NF - 1):
                at = HO + i * (2 * NF - i - 1) // 2
                src = Wc[at:at + NF - 1 - i, :].rearrange("a o -> o a").to_broadcast([DK, NF - 1 - i])
                sp.dma_start(c_raw[DK * i:DK * i + DK, i + 1:NF], src).then_inc(c_loaded, 16)
            reload_x(sp, 1, 1, (0, 1), x_first, HALVES[0])
            reload_x(sp, 2, 1, (0, 1), x_loaded, HALVES[1])
            with sp.Fori(2, TILES) as n:
                reload_x(sp, n + 1, n, (0, 1))
            reload_x(sp, V_B, 0, (0, 1))
            sp.wait_ge(c_split, 2)
            for k in range(KT):
                load_w1(1, k)
            with sp.Fori(1, TILES) as n:
                reload_x(sp, n + V_B, n, (0, 1))
            sp.wait_ge(turned, V_END * KT)
            sp.dma_start(w2_raw, W2.rearrange("(k p) n -> p k n", p=P)).then_inc(w2_loaded, 16)
            sp.wait_ge(x_lo, V_END * KT)
            sp.dma_start(w3, W3.rearrange("(m p) h -> p m h", p=P)).then_inc(l3_loaded, 16)
            sp.dma_start(wc_b, Wc[0:HO, :].rearrange("a o -> o a").to_broadcast([P, HO])).then_inc(l3_loaded, 16)
            sp.dma_start(b3_b, b3.rearrange("(o a) -> o a", o=1).to_broadcast([P, HO])).then_inc(l3_loaded, 16)
            sp.dma_start(bc_b[:, :], bc.rearrange("(o a) -> o a", o=1).to_broadcast([P, 1])).then_inc(l3_loaded, 16)
            sp.wait_ge(y_ready, TILES)
            sp.dma_start(out.rearrange("(o c) e -> o (c e)", o=1),
                         y_sb.rearrange("o n c -> o (n c)")).then_inc(y_stored, 16)
            sp.wait_ge(y_stored, 16)

        @block.gpsimd
        def _(pool):
            pool.memset(c_raw[:, :], 0.0).then_inc(pool_set, 1)
            pool.memset(ones[:, :], 1.0).then_inc(pool_set, 1)
            pool.memset(ident, 0.0).then_inc(pool_set, 1)
            pool.wait_ge(pool_set, 3)
            pool.affine_select(out=ident, in_=ident, compare_op=ALU.not_equal, fill=1.0, base=0,
                               pattern=[[-1, P]], channel_multiplier=1).then_inc(pool_set, 1)

            def lo_of_w1(s, k):
                pool.wait_ge(w_loaded[k], 16 * (s + 1))
                pool.wait_ge(w_hi, s * KT + k + 1)
                if s:
                    pool.wait_ge(pe_steps, (V_B - 1) * KT + k + 1)
                pool.tensor_tensor(w_hl[:, k, 1, :], w_stage(s, k),
                                   w_hl[:, k, 0, :].bitcast(FP32), ALU.subtract).then_inc(w_lo, 1)

            def x_plus_lo(v, k):
                pool.wait_ge(x_lo, v * KT + k + 1)
                pool.tensor_tensor(turned_slot(True, k), turned_slot(True, k),
                                   x_hl[:, k % HL_SLOTS, 1, :].bitcast(FP32), ALU.add).then_inc(x_plus, 1)

            for k in range(KT):
                lo_of_w1(0, k)
            with pool.Fori(1, TILES) as n:
                for k in range(KT):
                    x_plus_lo(n + 1, k)
            for k in range(KT):
                lo_of_w1(1, k)
                x_plus_lo(V_B, k)

        @block.scalar
        def _(act):
            load_x(act, 0, (2, 3), x_first, HALVES[0])
            act.wait_ge(pool_set, 2)
            act.copy(warm[:, :], ones[:, 0:1])

            def hi_of_w1(s, k):
                act.wait_ge(w_loaded[k], 16 * (s + 1))
                if s:
                    act.wait_ge(pe_steps, (V_B - 1) * KT + k + 1)
                act.copy(w_hl[:, k, 0, :], w_stage(s, k)).then_inc(w_hi, 1)

            def hi_of_x(v, k, many, cols=slice(0, NT), first=False):
                act.wait_ge(turned, v * KT + k + 1)
                if not (first and k < HL_SLOTS):
                    act.wait_ge(pe_steps, v * KT + k - HL_SLOTS + 1)
                act.copy(x_hl[:, k % HL_SLOTS, 0, cols], turned_slot(many, k)[:, cols]).then_inc(x_hi, 1)

            def relu1(s, v, n):
                if s:
                    act.wait_ge(prod_done, TILES * KT - LAG + 1)
                for m in range(MT):
                    if m < MT - 1:
                        act.wait_ge(m_done, (v - 2) * (MT - 1) + m + 1)
                    else:
                        act.wait_ge(pe_steps, v * KT)
                    act.activation(h1[:, s * MT + m, n, :], ps[m][:, :], ACT.Relu,
                                   bias=b1_c[:, s * MT + m:s * MT + m + 1]).then_inc(h1_ready, 1)

            def root(n):
                act.wait_ge(ve_ready, n + 1)
                act.activation(sd[:, 0:VE[n]], ve[:, 0:VE[n]], ACT.Sqrt).then_inc(sd_ready, 1)

            def hi_of_w2(k):
                act.wait_ge(a1_ready, 1 + k // (K2 // 2))
                act.wait_ge(w2_loaded, 16)
                act.wait_ge(pe_steps, (V_END - 1) * KT + k + 1)
                act.activation(w_hl[:, k, 0, :], w2_raw[:, k, :], ACT.Copy, scale=a1[:, k:k + 1]).then_inc(w2_hi, 1)

            def hi_of_h1(n, k, first):
                if first:
                    act.wait_ge(pe_steps, (V_END - 1) * KT + K2 + k + 1)
                    if k >= K2 // 2:
                        act.wait_ge(h1_ready, 2 * TILES * MT)
                else:
                    act.wait_ge(pe_steps2, (n - 1) * K2 + k + 1)
                act.copy(w_hl[:, K2 + k, 0, :], h1[:, k, n, :]).then_inc(h_hi, 1)

            def relu2(n):
                for m in range(M2):
                    if m < M2 - 1:
                        act.wait_ge(m2_done, n * (M2 - 1) + m + 1)
                    else:
                        act.wait_ge(pe_steps2, (n + 1) * K2)
                    act.activation(h2[:, m, n, :], ps[m][:, :], ACT.Relu, bias=b2f[:, m:m + 1]).then_inc(h2_ready, 1)

            def tile1(s, v, n, n_next):
                many = s == 0
                for k in range(KT):
                    if k == HL_SLOTS - 1:
                        relu1(s, v, n - 1)
                    hi_of_x(v, k, many)
                    if k == TURNED_EARLY + 1 and n_next is not None:
                        reload_x(act, v + 1, n_next, (2, 3))
                    if n_next is None and k == TURNED_EARLY:
                        root(0)
                    if n_next is None and k in AT_W2:
                        hi_of_w2(AT_W2.index(k))

            for k in range(KT):
                hi_of_w1(0, k)
                if k == TURNED_EARLY - 2:
                    load_x(act, 0, (2, 3), x_loaded, HALVES[1])
                hi_of_x(0, k, True, slice(0, HB), first=True)
                if k == HALF1_AT + 1:
                    reload_x(act, 1, 1, (2, 3), x_first, HALVES[0])
            for k in range(KT):
                hi_of_x(1, k, True, slice(HB, NT))
                if k == HL_SLOTS + 1:
                    reload_x(act, 2, 1, (2, 3), x_loaded, HALVES[1])
                if k == KT - 2:
                    act.wait_ge(c_built, 2)
                    act.copy(c_hl[:, 0, :], c_full[:, :, :].rearrange("p j e -> p (j e)")).then_inc(c_split, 1)
            act.wait_ge(par_ready, 1)
            act.wait_ge(w_lo, KT)
            with act.Fori(1, TILES - 1) as n:
                tile1(0, n + 1, n, n + 1)
            tile1(0, V_B - 1, TILES - 1, 0)
            for k in range(KT):
                if k == HL_SLOTS - 1:
                    relu1(0, V_B, TILES - 1)
                hi_of_w1(1, k)
                hi_of_x(V_B, k, True)
                if k == TURNED_EARLY + 1:
                    reload_x(act, V_B + 1, 1, (2, 3))
            act.wait_ge(w_lo, 2 * KT)
            with act.Fori(1, TILES - 1) as n:
                tile1(1, n + V_B, n, n + 1)
            tile1(1, V_END - 1, TILES - 1, None)
            for k in range(K2 // 2):
                hi_of_h1(0, k, True)
            relu1(1, V_END, TILES - 1)
            for k in range(K2 // 2, K2):
                hi_of_h1(0, k, True)
            root(1)
            for k in range(K2 // 2, K2):
                hi_of_w2(k)
            with act.Fori(1, TILES) as n:
                for k in range(K2):
                    if k == K2 - 1:
                        act.wait_ge(b2_ready, 1)
                        relu2(n - 1)
                    hi_of_h1(n, k, False)
            for m in range(M2):
                act.wait_ge(m2_done, (TILES - 1) * (M2 - 1) + m + 1)
                act.activation(h2[:, m, TILES - 1, :], ps[m][:, :], ACT.Relu, bias=b2f[:, m:m + 1]).then_inc(h2_ready, 1)
                root(2 + m)
            act.wait_ge(kc_ready, 1)
            for n in range(1, TILES, 2):
                act.wait_ge(y_done, n + 1)
                act.activation(y_sb[:, n, :].rearrange("o (j g) -> o g j", g=BLKS), by_rows(ps_y[n]), ACT.Identity,
                               bias=kc[0:1, 0:1]).then_inc(y_ready, 1)

        @block.tensor
        def _(pe):
            def three(acc, w_hi_ap, w_lo_ap, x_hi_ap, x_lo_ap, start, stop):
                pe.matmul(acc, w_hi_ap, x_hi_ap, start=start, stop=False)
                pe.matmul(acc, w_hi_ap, x_lo_ap, start=False, stop=False)
                return pe.matmul(acc, w_lo_ap, x_hi_ap, start=False, stop=stop)

            def tile1(s, v, pairs=None, cols=slice(0, NT), weights_new=False, reuse_banks=True, turn_c=False):
                for k in range(KT):
                    hi, lo = x_hl[:, k % HL_SLOTS, 0, cols], x_hl[:, k % HL_SLOTS, 1, cols]
                    pe.wait_ge(x_hi, v * KT + k + 1)
                    pe.wait_ge(x_lo, v * KT + k + 1)
                    if weights_new:
                        pe.wait_ge(w_hi, s * KT + k + 1)
                        pe.wait_ge(w_lo, s * KT + k + 1)
                    for m in range(MT):
                        if k == 0 and reuse_banks:
                            pe.wait_ge(h1_ready, (v - 2) * MT + m + 1)
                        wc = slice(m * P, (m + 1) * P)
                        mm = three(ps[m][:, cols], w_hl[:, k, 0, wc], w_hl[:, k, 1, wc], hi, lo, k == 0, k == KT - 1)
                        if k == KT - 1 and m < MT - 1 and cols.stop == NT:
                            mm.then_inc(m_done, 1)
                    if pairs is not None:
                        if not isinstance(pairs, int) or pairs or k >= 2:
                            pe.wait_ge(prod_done, pairs * KT + k - 1)
                        elif k == 0:
                            pe.wait_ge(c_split, 2)
                        pe.matmul(ps[4 + k % 2][:, :], c_hl[:, 0, :], hi, start=True, stop=False)
                        mm = pe.matmul(ps[4 + k % 2][:, :], c_hl[:, 1, :], hi, start=False, stop=True)
                    mm.then_inc(pe_steps, 1)
                    if turn_c and k == C_AT + 1:
                        pe.wait_ge(c_built, 1)
                        pe.transpose(ps_c, c_full[:, :, :].rearrange("p j e -> p (j e)"), ident).then_inc(c_turned, 1)

            pe.wait_ge(pool_set, 2)
            pe.wait_ge(w_loaded[0], 16)
            for _ in range(WARM_UP):
                pe.matmul(ps[7][:, 0:P], ones[:, :], ones[:, :], start=True, stop=True)
            tile1(0, 0, cols=slice(0, HB), weights_new=True, reuse_banks=False)
            pe.wait_ge(pool_set, 4)
            pe.wait_ge(par_loaded, 96)
            pe.transpose(ps_par, par_rows, ident[0:NPAR, 0:NPAR]).then_inc(par_turned, 1)
            tile1(0, 1, cols=slice(HB, NT), reuse_banks=False, turn_c=True)
            tile1(0, 2, pairs=0)
            with pe.Fori(2, TILES) as n:
                tile1(0, n + 1, pairs=n - 1)
            tile1(1, V_B, pairs=TILES - 1, weights_new=True)
            with pe.Fori(1, TILES) as n:
                tile1(1, n + V_B)

            def step2(n, k, first, m_from=0, m_to=M2):
                pe.wait_ge(h_hi, n * K2 + k + 1)
                pe.wait_ge(h_lo, n * K2 + k + 1)
                if first:
                    pe.wait_ge(w2_hi, k + 1)
                    pe.wait_ge(w2_lo, k + 1)
                for m in range(m_from, m_to):
                    if k == 0:
                        if first:
                            pe.wait_ge(h1_ready, (2 * TILES - 1) * MT + m + 1)
                        else:
                            pe.wait_ge(h2_ready, (n - 1) * M2 + m + 1)
                    cols = slice(m * P, (m + 1) * P)
                    mm = three(ps[m][:, :], w_hl[:, k, 0, cols], w_hl[:, k, 1, cols],
                               w_hl[:, K2 + k, 0, :], w_hl[:, K2 + k, 1, :], k == 0, k == K2 - 1)
                    if k == K2 - 1 and (m < M2 - 1 or m_from):
                        mm.then_inc(m2_done, 1)
                    elif m == M2 - 1 and not m_from:
                        mm.then_inc(pe_steps2, 1)

            for k in range(K2):
                step2(0, k, True)
                if k == K2 - 2:
                    pe.wait_ge(c1w2_added, K2)
                    for m in range(M2):
                        mm = pe.matmul(ps_b2[:, m:m + 1], c1w2[:, m * P:(m + 1) * P], ones[:, 0:1],
                                       start=True, stop=True)
                    mm.then_inc(b2_done, 1)
            with pe.Fori(1, TILES - 1) as n:
                for k in range(K2):
                    step2(n, k, False)
            for m in range(M2):
                for k in range(K2):
                    step2(TILES - 1, k, False, m, m + 1)
            for n in range(TILES):
                pe.wait_ge(h2_added, M2 - 2 + n + 1)
                pe.matmul(ps_y[n], ones[:, 0:1], sum_in[:, n, :], start=True, stop=False)
            pe.wait_ge(v2_ready, 1)
            for n in range(TILES):
                pe.matmul(ps_y[n], v2[:, M2 - 1:M2], h2[:, M2 - 1, n, :], start=False, stop=True).then_inc(y_done, 1)
                if n == 0:
                    pe.wait_ge(s2_ready, 1)
                    pe.matmul(ps_k, s2s[:, 0:1], ones[:, 0:1], start=True, stop=True).then_inc(k_done, 1)

        @block.vector
        def _(dve):
            chain = [0]

            def link(ins):
                chain[0] += 1
                ins.then_inc(dve_chain, 1)
                dve.wait_ge(dve_chain, chain[0])

            def build_c():
                dve.wait_ge(pool_set, 4)
                link(dve.tensor_reduce(c_mask[:, :], ident.rearrange("p (i e) -> p e i", e=DK), AX.X, ALU.max))
                dve.wait_ge(c_loaded, 16 * (NF - 1))
                for e in range(DK):
                    last = dve.tensor_scalar(c_full[:, :, e], c_raw[:, :], c_mask[:, e:e + 1], 0.5, ALU.mult, ALU.mult)
                last.then_inc(c_built, 1)

            def add_transpose_of_c():
                dve.wait_ge(c_turned, 1)
                c_rows = c_full[:, :, :].rearrange("p j e -> p (j e)")
                dve.tensor_tensor(c_rows, c_rows, ps_c, ALU.add).then_inc(c_built, 1)
                dve.wait_ge(c_split, 1)
                dve.tensor_tensor(c_hl[:, 1, :], c_full[:, :, :].rearrange("p j e -> p (j e)"),
                                  c_hl[:, 0, :].bitcast(FP32), ALU.subtract).then_inc(c_split, 1)

            def turn(v, k, many, half=None, reused=True, pairs_prev=None, new_halves=False):
                if k == 0:
                    if half == 0:
                        dve.wait_ge(x_first, 64)
                    else:
                        dve.wait_ge(x_loaded, v * 64)
                        if new_halves:
                            dve.wait_ge(x_first, 128)
                if not many and k >= XT_SLOTS:
                    dve.wait_ge(x_lo, v * KT + k - XT_SLOTS + 1)
                elif reused:
                    dve.wait_ge(x_lo, (v - 1) * KT + (k if many or pairs_prev is not None else k + XT_SLOTS) + 1)
                    if pairs_prev is not None:
                        dve.wait_ge(prod_done, pairs_prev * KT + k + 1)
                g = slice(0, BLKS) if half is None else slice(half * BLKS // 2, (half + 1) * BLKS // 2)
                cols = slice(g.start * 32, g.stop * 32)
                dve.transpose(turned_slot(many, k)[:, cols],
                              x_raw[:, g, :].rearrange("p b (i d) -> p b i d", d=D)[:, :, :, DK * k:DK * k + DK]
                              ).then_inc(turned, 1)

            def lo_of_x(v, k, many, cols, first, pairs=None, k_before=None):
                if pairs is not None:
                    dve.wait_ge(x_plus, pairs * KT + k_before + 1)
                dve.wait_ge(x_hi, v * KT + k + 1)
                if not (first and k < HL_SLOTS):
                    dve.wait_ge(pe_steps, v * KT + k - HL_SLOTS + 1)
                dve.tensor_tensor(x_hl[:, k % HL_SLOTS, 1, cols], turned_slot(many, k)[:, cols],
                                  x_hl[:, k % HL_SLOTS, 0, cols].bitcast(FP32), ALU.subtract).then_inc(x_lo, 1)

            def product(v, n, pairs, k):
                dve.wait_ge(pe_steps, v * KT + k + 1)
                if k > PROD or not (isinstance(pairs, int) and pairs == 0):
                    dve.wait_ge(sum_done, pairs * (KT - 1) + max(k - PROD, 0))
                dve.wait_ge(x_plus, pairs * KT + k + 1)
                dst = ps_sum if k == 0 else pair_prod[:, k % PROD, :]
                dve.tensor_tensor(dst, ps[4 + k % 2][:, :], turned_slot(True, k), ALU.mult).then_inc(prod_done, 1)

            def add_up(n, pairs, k):
                dve.wait_ge(prod_done, pairs * KT + k + 1)
                if k >= 2:
                    dve.wait_ge(sum_done, pairs * (KT - 1) + k - 1)
                dve.tensor_tensor(ps_sum if k < KT - 1 else sum_in[:, n, :], ps_sum, pair_prod[:, k % PROD, :],
                                  ALU.add).then_inc(sum_done, 1)

            def stats1(s, v, n, m):
                dve.wait_ge(h1_ready, (v - 2) * MT + m + 1)
                dve.bn_stats(st1[:, s * MT + m, n, :], h1[:, s * MT + m, n, :]).then_inc(st1_done, 1)

            def tile1(v, many, half=None, now=None, before=None, stats=None, many_next=True, last=False,
                      turned_before=1):
                cols = slice(0, NT) if half is None else slice(half * HB, (half + 1) * HB)
                for k in range(KT):
                    if k < LAG and before:
                        lo_of_x(v, k, many, cols, half == 0, before[1], KT + k - LAG)
                        product(v - 1, *before, KT + k - LAG)
                    elif k >= LAG and now:
                        lo_of_x(v, k, many, cols, half == 0, now[1], k - LAG)
                        if k == LAG and before:
                            add_up(*before, KT - 1)
                        product(v, *now, k - LAG)
                    else:
                        lo_of_x(v, k, many, cols, half == 0)
                        if k == LAG and before:
                            add_up(*before, KT - 1)
                    for kk in (2 * k + 1, 2 * k + 2):
                        if turned_before <= kk < KT and half != 1:
                            turn(v, kk, many, half, half is None, before and before[1])
                    if half == 0 and k >= HALF1_AT or half == 1:
                        at = (k - HALF1_AT if half == 0 else k + KT - HALF1_AT) * TURN_HALF
                        for kk in range(at, min(at + TURN_HALF, KT)):
                            turn(1, kk, True, 1, False)
                    if half == 1 and k >= KT - 3:
                        turn(v + 1, k - KT + 3, True, new_halves=True)
                    elif half is None and k == KT - 1 and not last:
                        turn(v + 1, 0, many_next, None, True, now and now[1])
                    if k < LAG and before:
                        add_up(*before, KT + k - LAG - 1)
                    if k >= LAG + 2 and now:
                        add_up(*now, k - LAG - 1)
                    if stats and HL_SLOTS <= k < HL_SLOTS + MT:
                        stats1(stats[0], v, stats[1], k - HL_SLOTS)
                    if half == 1 and k == KT // 2:
                        dve.wait_ge(par_turned, 1)
                        dve.tensor_copy(par[:, :], ps_par).then_inc(par_ready, 1)
                    if half == 1 and k == C_AT:
                        build_c()
                    if half == 1 and k == KT - 2:
                        add_transpose_of_c()
                    if last and k < MT:
                        aggregate1(k)
                    if last and k == TURNED_EARLY:
                        fold_scale(g1_c, be1_c, mv1, a1, c1, 0, MT, 0).then_inc(a1_ready, 1)
                    if last and k in AT_W2:
                        lo_of_w2(AT_W2.index(k))
                        add_c1w2(AT_W2.index(k))

            def aggregate1(m):
                dve.wait_ge(st1_done, (m // MT + 1) * TILES * MT)
                link(dve.bn_aggr(mv1[:, m, :], st1[:, m, :, :].rearrange("p t s -> p (t s)")))

            def fold_scale(g, be, mv, a, c, lo, hi, batch):
                w = hi - lo
                dve.tensor_scalar(ve[:, 0:w], mv[:, lo:hi, 1], EPS, None, ALU.add).then_inc(ve_ready, 1)
                dve.wait_ge(sd_ready, batch + 1)
                link(dve.reciprocal(r0[:, 0:w], sd[:, 0:w]))
                link(dve.tensor_tensor(nt[:, 0:w], r0[:, 0:w], r0[:, 0:w], ALU.mult))
                link(dve.tensor_tensor(nt[:, 0:w], nt[:, 0:w], ve[:, 0:w], ALU.mult))
                link(dve.tensor_scalar(nt[:, 0:w], nt[:, 0:w], -0.5, 1.5, ALU.mult, ALU.add))
                link(dve.tensor_tensor(nt[:, 0:w], nt[:, 0:w], r0[:, 0:w], ALU.mult))
                link(dve.tensor_tensor(a[:, lo:hi], nt[:, 0:w], g[:, lo:hi], ALU.mult))
                link(dve.tensor_tensor(nt[:, 0:w], mv[:, lo:hi, 0], a[:, lo:hi], ALU.mult))
                return dve.tensor_tensor(c[:, lo:hi], be[:, lo:hi], nt[:, 0:w], ALU.subtract)

            def lo_of_w2(k):
                dve.wait_ge(w2_hi, k + 1)
                dve.scalar_tensor_tensor(w_hl[:, k, 1, :], w2_raw[:, k, :], a1[:, k:k + 1],
                                         w_hl[:, k, 0, :].bitcast(FP32), ALU.mult, ALU.subtract).then_inc(w2_lo, 1)

            def add_c1w2(k):
                if k == 0:
                    ins = dve.tensor_scalar(c1w2, w2_raw[:, 0, :], c1[:, 0:1], None, ALU.mult)
                else:
                    dve.wait_ge(c1w2_added, k)
                    ins = dve.scalar_tensor_tensor(c1w2, w2_raw[:, k, :], c1[:, k:k + 1], c1w2, ALU.mult, ALU.add)
                ins.then_inc(c1w2_added, 1)

            def lo_of_h1(n, k):
                dve.wait_ge(h_hi, n * K2 + k + 1)
                dve.tensor_tensor(w_hl[:, K2 + k, 1, :], h1[:, k, n, :], w_hl[:, K2 + k, 0, :].bitcast(FP32),
                                  ALU.subtract).then_inc(h_lo, 1)

            turn(0, 0, True, 0, False)
            tile1(0, True, half=0)
            tile1(1, True, half=1)
            tile1(2, True, now=(1, 0), stats=(0, 0), turned_before=3)
            with dve.Fori(2, TILES) as n:
                tile1(n + 1, True, now=(n, n - 1), before=(n - 1, n - 2), stats=(0, n - 1))
            tile1(V_B, True, now=(0, TILES - 1), before=(TILES - 1, TILES - 2), stats=(0, TILES - 1), many_next=False)
            tile1(V_B + 1, False, before=(0, TILES - 1), stats=(1, 0), many_next=False)
            with dve.Fori(2, TILES - 1) as n:
                tile1(n + V_B, False, stats=(1, n - 1), many_next=False)
            tile1(V_END - 1, False, stats=(1, TILES - 2), last=True)
            for k in range(K2 // 2):
                lo_of_h1(0, k)
            for m in range(MT):
                stats1(1, V_END, TILES - 1, m)
            for m in range(MT, K2):
                aggregate1(m)
            fold_scale(g1_c, be1_c, mv1, a1, c1, MT, K2, 1).then_inc(a1_ready, 1)
            for k in range(K2 // 2, K2):
                lo_of_w2(k)
                lo_of_h1(0, k)
            for k in range(K2 // 2, K2):
                add_c1w2(k)
            dve.wait_ge(b2_done, 1)
            dve.tensor_tensor(b2f[:, :], ps_b2, b2_c, ALU.add).then_inc(b2_ready, 1)

            def stats2(n, m):
                dve.wait_ge(h2_ready, n * M2 + m + 1)
                return dve.bn_stats(st2[:, m, n, :], h2[:, m, n, :])

            with dve.Fori(1, TILES) as n:
                for k in range(K2 - 1):
                    lo_of_h1(n, k)
                for m in range(M2):
                    stats2(n - 1, m)
                lo_of_h1(n, K2 - 1)

            dve.wait_ge(l3_loaded, 64)
            wc_m = wc_b.rearrange("p (m h) -> p m h", m=1).to_broadcast([P, M2, HO])
            link(dve.tensor_tensor(w3p, w3, wc_m, ALU.mult))
            link(dve.tensor_reduce(w3c[:, :], w3p, AX.X, ALU.add))
            link(dve.tensor_tensor(b3p, b3_b, wc_b, ALU.mult))
            link(dve.tensor_reduce(k3[:, :], b3p, AX.X, ALU.add))
            link(dve.tensor_tensor(k3[:, :], k3[:, :], bc_b[:, :], ALU.add))
            link(dve.tensor_tensor(gw[:, :], g2_c, w3c[:, :], ALU.mult))
            link(dve.tensor_tensor(bw[:, :], be2_c, w3c[:, :], ALU.mult))
            for m in range(M2):
                link(stats2(TILES - 1, m))
                link(dve.bn_aggr(mv2[:, m, :], st2[:, m, :, :].rearrange("p t s -> p (t s)")))
                dve.tensor_scalar(ve[:, 0:1], mv2[:, m, 1:2], EPS, None, ALU.add).then_inc(ve_ready, 1)
                dve.wait_ge(sd_ready, 3 + m)
                link(dve.reciprocal(r0[:, 0:1], sd[:, 0:1]))
                link(dve.tensor_scalar(nt[:, 0:1], r0[:, 0:1], r0[:, 0:1], ve[:, 0:1], ALU.mult, ALU.mult))
                link(dve.tensor_scalar(nt[:, 0:1], nt[:, 0:1], -0.5, 1.5, ALU.mult, ALU.add))
                dve.tensor_scalar(v2[:, m:m + 1], nt[:, 0:1], r0[:, 0:1], gw[:, m:m + 1], ALU.mult,
                                  ALU.mult).then_inc(v2_ready if m == M2 - 1 else dve_chain, 1)
                if m == M2 - 1:
                    dve.wait_ge(v2_ready, 1)
                else:
                    chain[0] += 1
                    dve.wait_ge(dve_chain, chain[0])
                    for at in [slice(0, TILES)] if m < M2 - 2 else [slice(n, n + 1) for n in range(TILES)]:
                        if m and at.start == 0:
                            dve.wait_ge(h2_added, m)
                        dve.scalar_tensor_tensor(row(sum_in[:, at, :]), row(h2[:, m, at, :]), v2[:, m:m + 1],
                                                 row(sum_in[:, at, :]), ALU.mult, ALU.add).then_inc(h2_added, 1)
                link(dve.tensor_scalar(s2[:, m:m + 1], mv2[:, m, 0:1], v2[:, m:m + 1], bw[:, m:m + 1],
                                       ALU.mult, ALU.subtract))
            dve.tensor_reduce(s2s[:, :], s2[:, :], AX.X, ALU.add).then_inc(s2_ready, 1)
            dve.wait_ge(k_done, 1)
            dve.tensor_tensor(kc[0:1, :], k3[0:1, :], ps_k, ALU.subtract).then_inc(kc_ready, 1)
            dve.wait_ge(kc_ready, 1)
            for n in range(0, TILES, 2):
                dve.wait_ge(y_done, n + 1)
                dve.tensor_scalar(y_sb[:, n, :].rearrange("o (j g) -> o g j", g=BLKS), by_rows(ps_y[n]), kc[0:1, 0:1],
                                  None, ALU.add).then_inc(y_ready, 1)


_INS = ['r_x', 'L0_rec_W1', 'L0_rec_b1', 'L0_rec_g1', 'L0_rec_beta1', 'L0_rec_W2', 'L0_rec_b2', 'L0_rec_g2',
        'L0_rec_beta2', 'L0_rec_W3', 'L0_rec_b3', 'L0_rec_Wc', 'L0_rec_bc']
_OUTS = [((B, 1), 'float32')]


def kernel(**inputs):
    import numpy as _np
    import concourse.bacc as _bacc
    from concourse import mybir as _mybir
    from concourse.bass_utils import run_bass_kernel_spmd as _run

    nc = _bacc.Bacc("TRN2", target_bir_lowering=False, num_devices=1)
    arrays, args = {}, []
    for name in _INS:
        a = _np.ascontiguousarray(inputs[name])
        arrays[f"in_{name}_dram"] = a
        args.append(nc.dram_tensor(f"in_{name}_dram", a.shape, _mybir.dt.from_np(a.dtype), kind="ExternalInput").ap())
    for i, (shape, dtype) in enumerate(_OUTS):
        dt = _mybir.dt.from_np(_np.dtype(dtype))
        args.append(nc.dram_tensor(f"out_{i}_dram", shape, dt, kind="ExternalOutput").ap())
    build(nc, *args)
    r = _run(nc, [arrays], core_ids=[0])
    got = tuple(r.results[0][f"out_{i}_dram"] for i in range(len(_OUTS)))
    return got[0]
```
